# Optimizing a Trainium2 kernel written in Bass

```python
import numpy as np
import jax
import jax.numpy as jnp

def _softmax(x, axis=-1):
    return jax.nn.softmax(x, axis=axis)

def _gelu(x):
    return jax.nn.gelu(x, approximate=True)

def _silu(x):
    return jax.nn.silu(x)

def _sigmoid(x):
    return jax.nn.sigmoid(x)

def _layernorm(x, axis=-1, eps=1e-05):
    m = jnp.mean(x, axis=axis, keepdims=True)
    v = jnp.var(x, axis=axis, keepdims=True)
    return (x - m) / jnp.sqrt(v + eps)

def _scatter_add(tgt, idx, src, axis=0):
    return tgt.at[idx].add(src)

def _segment_sum(src, seg, n):
    return jax.ops.segment_sum(src, seg, n)
kernel_name = 'mk_xattn_seq_d2_seqx_r8_13e8ea'

def setup_inputs(seed: int=0):
    np.random.seed(seed)
    _w = jnp.asarray

    def _rec_inputs():
        import jax
        import jax.numpy as jnp
        _rk = jax.random.key(seed)
        x = 7.22e-05 + 1 * jax.random.normal(jax.random.fold_in(_rk, 1), (4, 256, 256), jnp.float32)
        _lenS = 256 - jax.random.randint(jax.random.fold_in(_rk, 7), (4,), 0, max(1, 256 // 4) + 1, jnp.int32)
        _lenS2 = 512 - jax.random.randint(jax.random.fold_in(_rk, 8), (4,), 0, max(1, 512 // 4) + 1, jnp.int32)
        _ctx_2048P = jax.random.normal(jax.random.fold_in(_rk, 11), (4, 16, 256), jnp.float32)
        _ctx_2048c = jax.random.dirichlet(jax.random.fold_in(_rk, 511), 0.3 * jnp.ones((16,), jnp.float32), (4, 512))
        _ctx_2048t = jnp.einsum('bsk,bkd->bsd', _ctx_2048c, _ctx_2048P)
        _ctx_2048t = _ctx_2048t * jax.lax.rsqrt(jnp.mean(jnp.square(_ctx_2048t)) + 1e-12) * 0.953939
        ctx_2048 = 4.13588e-05 + 0.999923 * (_ctx_2048t + 0.3 * jax.random.normal(jax.random.fold_in(_rk, 611), (4, 512, 256), jnp.float32))
        _validS = jnp.arange(256)[None, :] < _lenS[:, None]
        _validS2 = jnp.arange(512)[None, :] < _lenS2[:, None]
        _causal = jnp.tril(jnp.ones((256, 256), dtype=bool))
        mask_Bx1xSxS2_ff0 = jnp.where(jnp.ones((4, 1, 256, 512), dtype=bool), 0.0, -1000000000.0).astype(jnp.float32)
        mask_BxS2_bf1 = jnp.ones((4, 512), dtype=bool)
        return (x, ctx_2048, mask_Bx1xSxS2_ff0, mask_BxS2_bf1)
    x, ctx_2048, mask_Bx1xSxS2_ff0, mask_BxS2_bf1 = _rec_inputs()

    def _L0_xattn_setup():
        import jax, jax.numpy as jnp
        import numpy as np
        H = 256
        NH = 32
        KVH = 8
        HD = H // NH
        GROUPS = NH // KVH
        EPS = 1e-06
        B, L, S = (4, 128, 128)

        def _gqa_forward(hidden_state, encoder_hidden_state, encoder_attention_mask, Wq, bq, Wk, bk, Wv, bv, Wo, bo, gamma, beta):
            b, l, _ = hidden_state.shape
            s = encoder_hidden_state.shape[1]
            q = hidden_state @ Wq + bq
            k = encoder_hidden_state @ Wk + bk
            v = encoder_hidden_state @ Wv + bv
            q = q.reshape(b, l, KVH, GROUPS, HD).transpose(0, 2, 3, 1, 4)
            k = k.reshape(b, s, KVH, HD).transpose(0, 2, 1, 3)
            v = v.reshape(b, s, KVH, HD).transpose(0, 2, 1, 3)
            scale = 1.0 / jnp.sqrt(jnp.asarray(HD, q.dtype))
            scores = jnp.einsum('bkgld,bksd->bkgls', q, k) * scale
            scores = scores + encoder_attention_mask[:, :, None, :, :]
            attn = jax.nn.softmax(scores, axis=-1)
            out = jnp.einsum('bkgls,bksd->bkgld', attn, v)
            out = out.transpose(0, 3, 1, 2, 4).reshape(b, l, H)
            out = out @ Wo + bo
            x = out + hidden_state
            mu = jnp.mean(x, axis=-1, keepdims=True)
            var = jnp.var(x, axis=-1, keepdims=True)
            return (x - mu) * jax.lax.rsqrt(var + EPS) * gamma + beta
        key = jax.random.key(seed)
        ks = jax.random.split(key, 12)
        sd = 0.02
        return {'hidden_state': jax.random.normal(ks[0], (B, L, H), jnp.float32), 'encoder_hidden_state': jax.random.normal(ks[1], (B, S, H), jnp.float32), 'encoder_attention_mask': jnp.zeros((B, 1, L, S), jnp.float32), 'Wq': jax.random.normal(ks[2], (H, H), jnp.float32) * sd, 'bq': jnp.zeros((H,), jnp.float32), 'Wk': jax.random.normal(ks[3], (H, KVH * HD), jnp.float32) * sd, 'bk': jnp.zeros((KVH * HD,), jnp.float32), 'Wv': jax.random.normal(ks[4], (H, KVH * HD), jnp.float32) * sd, 'bv': jnp.zeros((KVH * HD,), jnp.float32), 'Wo': jax.random.normal(ks[5], (H, H), jnp.float32) * sd, 'bo': jnp.zeros((H,), jnp.float32), 'gamma': jnp.ones((H,), jnp.float32), 'beta': jnp.zeros((H,), jnp.float32)}
    _L0_xattn_all = _L0_xattn_setup()
    _L0_xattn_in = {k: v for k, v in _L0_xattn_all.items() if k in ('Wq', 'bq', 'Wk', 'bk', 'Wv', 'bv', 'Wo', 'bo', 'gamma', 'beta')}
    del _L0_xattn_all

    def _L1_xattn_setup():
        import jax, jax.numpy as jnp
        import numpy as np
        D = 256
        H = 16
        HD = D // H
        INNER = 4 * D
        EPS = 1e-05

        def layer_norm(x, w, b):
            mu = jnp.mean(x, axis=-1, keepdims=True)
            var = jnp.mean(jnp.square(x - mu), axis=-1, keepdims=True)
            return (x - mu) * jax.lax.rsqrt(var + EPS) * w + b
        key = jax.random.key(seed)
        ks = jax.random.split(key, 12)
        B, LQ, LK = (4, 128, 256)
        std = 0.02
        inp = {'hidden_states': jax.random.normal(ks[0], (B, LQ, D), jnp.float32), 'encoder_hidden_states': jax.random.normal(ks[1], (B, LK, D), jnp.float32), 'encoder_attention_mask': jnp.ones((B, LK), dtype=bool), 'ln1_w': jnp.ones((D,), jnp.float32), 'ln1_b': jnp.zeros((D,), jnp.float32), 'q_w': jax.random.normal(ks[2], (D, D), jnp.float32) * std, 'q_b': jnp.zeros((D,), jnp.float32), 'k_w': jax.random.normal(ks[3], (D, D), jnp.float32) * std, 'k_b': jnp.zeros((D,), jnp.float32), 'v_w': jax.random.normal(ks[4], (D, D), jnp.float32) * std, 'v_b': jnp.zeros((D,), jnp.float32), 'cproj_w': jax.random.normal(ks[5], (D, D), jnp.float32) * std, 'cproj_b': jnp.zeros((D,), jnp.float32), 'ln2_w': jnp.ones((D,), jnp.float32), 'ln2_b': jnp.zeros((D,), jnp.float32), 'fc_w': jax.random.normal(ks[6], (D, INNER), jnp.float32) * std, 'fc_b': jnp.zeros((INNER,), jnp.float32), 'proj_w': jax.random.normal(ks[7], (INNER, D), jnp.float32) * std, 'proj_b': jnp.zeros((D,), jnp.float32)}
        return inp
    _L1_xattn_all = _L1_xattn_setup()
    _L1_xattn_in = {k: v for k, v in _L1_xattn_all.items() if k in ('ln1_w', 'ln1_b', 'q_w', 'q_b', 'k_w', 'k_b', 'v_w', 'v_b', 'cproj_w', 'cproj_b', 'ln2_w', 'ln2_b', 'fc_w', 'fc_b', 'proj_w', 'proj_b')}
    del _L1_xattn_all
    return {'x': x, 'ctx_2048': ctx_2048, 'mask_Bx1xSxS2_ff0': mask_Bx1xSxS2_ff0, 'mask_BxS2_bf1': mask_BxS2_bf1, 'L0_xattn_Wq': _L0_xattn_in['Wq'], 'L0_xattn_bq': _L0_xattn_in['bq'], 'L0_xattn_Wk': _L0_xattn_in['Wk'], 'L0_xattn_bk': _L0_xattn_in['bk'], 'L0_xattn_Wv': _L0_xattn_in['Wv'], 'L0_xattn_bv': _L0_xattn_in['bv'], 'L0_xattn_Wo': _L0_xattn_in['Wo'], 'L0_xattn_bo': _L0_xattn_in['bo'], 'L0_xattn_gamma': _L0_xattn_in['gamma'], 'L0_xattn_beta': _L0_xattn_in['beta'], 'L1_xattn_ln1_w': _L1_xattn_in['ln1_w'], 'L1_xattn_ln1_b': _L1_xattn_in['ln1_b'], 'L1_xattn_q_w': _L1_xattn_in['q_w'], 'L1_xattn_q_b': _L1_xattn_in['q_b'], 'L1_xattn_k_w': _L1_xattn_in['k_w'], 'L1_xattn_k_b': _L1_xattn_in['k_b'], 'L1_xattn_v_w': _L1_xattn_in['v_w'], 'L1_xattn_v_b': _L1_xattn_in['v_b'], 'L1_xattn_cproj_w': _L1_xattn_in['cproj_w'], 'L1_xattn_cproj_b': _L1_xattn_in['cproj_b'], 'L1_xattn_ln2_w': _L1_xattn_in['ln2_w'], 'L1_xattn_ln2_b': _L1_xattn_in['ln2_b'], 'L1_xattn_fc_w': _L1_xattn_in['fc_w'], 'L1_xattn_fc_b': _L1_xattn_in['fc_b'], 'L1_xattn_proj_w': _L1_xattn_in['proj_w'], 'L1_xattn_proj_b': _L1_xattn_in['proj_b']}

def reference(x, ctx_2048, mask_Bx1xSxS2_ff0, mask_BxS2_bf1, L0_xattn_Wq, L0_xattn_bq, L0_xattn_Wk, L0_xattn_bk, L0_xattn_Wv, L0_xattn_bv, L0_xattn_Wo, L0_xattn_bo, L0_xattn_gamma, L0_xattn_beta, L1_xattn_ln1_w, L1_xattn_ln1_b, L1_xattn_q_w, L1_xattn_q_b, L1_xattn_k_w, L1_xattn_k_b, L1_xattn_v_w, L1_xattn_v_b, L1_xattn_cproj_w, L1_xattn_cproj_b, L1_xattn_ln2_w, L1_xattn_ln2_b, L1_xattn_fc_w, L1_xattn_fc_b, L1_xattn_proj_w, L1_xattn_proj_b):
    import jax
    import jax.numpy as jnp

    def _L0_xattn_ref(hidden_state, encoder_hidden_state, encoder_attention_mask, Wq, bq, Wk, bk, Wv, bv, Wo, bo, gamma, beta):
        import jax, jax.numpy as jnp
        import numpy as np
        H = 256
        NH = 32
        KVH = 8
        HD = H // NH
        GROUPS = NH // KVH
        EPS = 1e-06
        B, L, S = (4, 128, 128)

        def _gqa_forward(hidden_state, encoder_hidden_state, encoder_attention_mask, Wq, bq, Wk, bk, Wv, bv, Wo, bo, gamma, beta):
            b, l, _ = hidden_state.shape
            s = encoder_hidden_state.shape[1]
            q = hidden_state @ Wq + bq
            k = encoder_hidden_state @ Wk + bk
            v = encoder_hidden_state @ Wv + bv
            q = q.reshape(b, l, KVH, GROUPS, HD).transpose(0, 2, 3, 1, 4)
            k = k.reshape(b, s, KVH, HD).transpose(0, 2, 1, 3)
            v = v.reshape(b, s, KVH, HD).transpose(0, 2, 1, 3)
            scale = 1.0 / jnp.sqrt(jnp.asarray(HD, q.dtype))
            scores = jnp.einsum('bkgld,bksd->bkgls', q, k) * scale
            scores = scores + encoder_attention_mask[:, :, None, :, :]
            attn = jax.nn.softmax(scores, axis=-1)
            out = jnp.einsum('bkgls,bksd->bkgld', attn, v)
            out = out.transpose(0, 3, 1, 2, 4).reshape(b, l, H)
            out = out @ Wo + bo
            x = out + hidden_state
            mu = jnp.mean(x, axis=-1, keepdims=True)
            var = jnp.var(x, axis=-1, keepdims=True)
            return (x - mu) * jax.lax.rsqrt(var + EPS) * gamma + beta
        return _gqa_forward(hidden_state, encoder_hidden_state, encoder_attention_mask, Wq, bq, Wk, bk, Wv, bv, Wo, bo, gamma, beta)

    def _L1_xattn_ref(hidden_states, encoder_hidden_states, encoder_attention_mask, ln1_w, ln1_b, q_w, q_b, k_w, k_b, v_w, v_b, cproj_w, cproj_b, ln2_w, ln2_b, fc_w, fc_b, proj_w, proj_b):
        import jax, jax.numpy as jnp
        import numpy as np
        D = 256
        H = 16
        HD = D // H
        INNER = 4 * D
        EPS = 1e-05

        def layer_norm(x, w, b):
            mu = jnp.mean(x, axis=-1, keepdims=True)
            var = jnp.mean(jnp.square(x - mu), axis=-1, keepdims=True)
            return (x - mu) * jax.lax.rsqrt(var + EPS) * w + b
        B, LQ, _ = hidden_states.shape
        LK = encoder_hidden_states.shape[1]
        residual = hidden_states
        x = layer_norm(hidden_states, ln1_w, ln1_b)
        q = (x @ q_w + q_b).reshape(B, LQ, H, HD).transpose(0, 2, 1, 3)
        k = (encoder_hidden_states @ k_w + k_b).reshape(B, LK, H, HD).transpose(0, 2, 1, 3)
        v = (encoder_hidden_states @ v_w + v_b).reshape(B, LK, H, HD).transpose(0, 2, 1, 3)
        scale = 1.0 / np.sqrt(HD).astype(np.float32)
        scores = jnp.einsum('bhqd,bhkd->bhqk', q, k) * scale
        mask = encoder_attention_mask[:, None, None, :]
        mask_value = jnp.finfo(scores.dtype).min
        scores = jnp.where(mask, scores, mask_value)
        attn = jax.nn.softmax(scores, axis=-1)
        out = jnp.einsum('bhqk,bhkd->bhqd', attn, v)
        out = out.transpose(0, 2, 1, 3).reshape(B, LQ, D)
        out = out @ cproj_w + cproj_b
        hidden = out + residual
        residual = hidden
        y = layer_norm(hidden, ln2_w, ln2_b)
        y = jax.nn.gelu(y @ fc_w + fc_b, approximate=True)
        y = y @ proj_w + proj_b
        return residual + y
    x = _L0_xattn_ref(x, ctx_2048, mask_Bx1xSxS2_ff0, L0_xattn_Wq, L0_xattn_bq, L0_xattn_Wk, L0_xattn_bk, L0_xattn_Wv, L0_xattn_bv, L0_xattn_Wo, L0_xattn_bo, L0_xattn_gamma, L0_xattn_beta)
    x = _L1_xattn_ref(x, ctx_2048, mask_BxS2_bf1, L1_xattn_ln1_w, L1_xattn_ln1_b, L1_xattn_q_w, L1_xattn_q_b, L1_xattn_k_w, L1_xattn_k_b, L1_xattn_v_w, L1_xattn_v_b, L1_xattn_cproj_w, L1_xattn_cproj_b, L1_xattn_ln2_w, L1_xattn_ln2_b, L1_xattn_fc_w, L1_xattn_fc_b, L1_xattn_proj_w, L1_xattn_proj_b)
    return x

_drawn_inputs = setup_inputs


def setup_inputs(seed=0):
    import zlib

    import numpy as np

    out = dict(_drawn_inputs(seed))
    spreads = {'L0_xattn_bq': (0.0, 0.8),
     'L0_xattn_bk': (0.0, 0.8),
     'L0_xattn_bv': (0.0, 0.1),
     'L0_xattn_bo': (0.0, 0.1),
     'L0_xattn_gamma': (1.0, 0.2),
     'L0_xattn_beta': (0.0, 0.1),
     'L1_xattn_ln1_w': (1.0, 0.6),
     'L1_xattn_ln1_b': (0.0, 0.8),
     'L1_xattn_q_b': (0.0, 0.8),
     'L1_xattn_k_b': (0.0, 0.8),
     'L1_xattn_v_b': (0.0, 0.277),
     'L1_xattn_cproj_b': (0.0, 0.1),
     'L1_xattn_ln2_w': (1.0, 0.6),
     'L1_xattn_ln2_b': (0.0, 0.8),
     'L1_xattn_fc_b': (0.0, 0.1),
     'L1_xattn_proj_b': (0.0, 0.1)}
    factors = {'L0_xattn_Wq': 8.0, 'L0_xattn_Wk': 8.0, 'L1_xattn_q_w': 8.0, 'L1_xattn_k_w': 8.0}
    for name, (base, spread) in spreads.items():
        noise = np.random.default_rng([zlib.crc32(name.encode()), seed]).standard_normal(out[name].shape)
        drawn = base * np.exp(spread * noise) if base else spread * noise
        out[name] = jnp.asarray(drawn.astype(out[name].dtype))
    for name, factor in factors.items():
        out[name] = (out[name] * factor).astype(out[name].dtype)
    return out
```

```python
from contextlib import ExitStack

import numpy as np

import concourse.bass as bass
from concourse import mybir

ALU = mybir.AluOpType
ACT = mybir.ActivationFunctionType
AX = mybir.AxisListType
F32 = mybir.dt.float32
BF16 = mybir.dt.bfloat16
I32 = mybir.dt.int32
U8 = mybir.dt.uint8

B, LQ, LK, D = 4, 256, 512, 256
P = 128
QT, KT, C = LQ // P, LK // P, D // P
INNER = 4 * D
FT = INNER // P
HD = (8, 16)
NH = (32, 16)
NG = (8, 16)
KF = tuple(g * d for g, d in zip(NG, HD))
UH = 8
NU = tuple(h // UH for h in NH)
STEPS = 4
BANKS = 4
LAG = 6
VW = 32
Q_PART = (0, 0, 0, 1, 1, 2)
K_PART = (0, 1, 2, 0, 1, 0)
PAIRS = len(Q_PART)
PROD = tuple(PAIRS * d for d in HD)
M_ROW = 96
MASK_ROW = M_ROW + 3
S_ROWS = (M_ROW, MASK_ROW + 1)
ST_ROWS = M_ROW + 3
CS = 4
SCALE = tuple(float(d) ** -0.5 for d in HD)
FAR = float(2.0 ** 127)
EPS = (1e-6, 1e-5, 1e-5)

UNITS = [(0, b, u) for b in range(B) for u in range(NU[0])] + [(1, b, u) for b in range(B) for u in range(NU[1])]
C0 = B * NU[0]
AS = NU[0] * STEPS
BS = NU[1] * STEPS
ALL = len(UNITS) * STEPS


def timeline():
    ops = []
    for n in ("k0", "q0", "v0", "v1", "v2", "v3"):
        ops.append((-1, n, 0))
    ops.append((-1, "flag", 0))
    ops += [(1, "k1_0", 0), (2, "k1_1", 0), (3, "c0", 0)]
    for b in range(1, B):
        for at, n in ((4, "k0"), (5, "q0"), (6, "v0"), (7, "v1"), (8, "v2"), (9, "v3"), (10, "k1_0"), (11, "k1_1")):
            ops.append(((b - 1) * AS + at, n, b))
    for g in range(len(UNITS)):
        ops.append((g * STEPS + STEPS, "m", g))
        ops.append((g * STEPS + STEPS - 1 + LAG + 2, "o", g))
    for b in range(B):
        end = b * AS + AS - 1 + LAG + 2
        ops += [(end + 1, "a0", b), (end + 2, "w0", b), (end + 5, "y1", b), (end + 6, "q1", b)]
        end = C0 * STEPS + b * BS + BS - 1 + LAG + 2
        ops += [(end + 1, "a1", b), (end + 2, "w1", b), (end + 4, "y2", b)]
        ops += [(end + 5, f"f{i}", b) for i in range(FT // 2)]
        ops += [(end + 6 + t, f"p{t}", b) for t in range(QT)]
    return sorted(ops, key=lambda o: o[0])


OPS = timeline()
AT = {(n, b): t for t, n, b in OPS}
PLACE = {(n, b): (i % 2, i // 2) for i, (_, n, b) in enumerate(OPS)}
END = max(AT.values()) + 1
SPLITS = [(AT[n, b], n, b, c) for _, n, b in OPS if n in ("k0", "q0", "k1_0", "k1_1", "q1")
          for c in range(2 if n[0] == "q" else 1)]
SPLIT = {(n, b, c): i for i, (_, n, b, c) in enumerate(SPLITS)}


def ops_at(t, names=None):
    return [(n, b) for s, n, b in OPS if s == t and (names is None or n in names)]


COL = {}
for _n, _w in (("bq0", C), ("bk0", 1), ("bv0", C), ("bq1", C), ("bk1", C), ("bv1", C), ("ln1w", C), ("ln1b", C),
               ("ln2w", C), ("ln2b", C), ("fcb", FT)):
    COL[_n] = (sum(w for _, w in COL.values()), _w)
NCOL = sum(w for _, w in COL.values())
ROW = {n: i for i, n in enumerate(("bo", "gamma", "beta", "cb", "pb"))}


def build(nc, xT, x, ctxT, mask, keymask, keymaskT, Wq0, Wk0, Wv, Wo0, Wq1, Wk1, Wc1, fcw, pjw, cols, rows, eye, out):
    with ExitStack() as ctx:
        def sb(name, shape, dt=F32):
            return ctx.enter_context(nc.sbuf_tensor(name, shape, dt))

        def sem(name):
            return ctx.enter_context(nc.semaphore(name))

        wq0 = sb("wq0", [P, C, D])
        wk0 = sb("wk0", [P, C, KF[0]])
        wv = sb("wv", [P, C, KF[0] + KF[1]])
        wo0 = sb("wo0", [P, C, D])
        wq1 = sb("wq1", [P, C, D])
        wk1 = sb("wk1", [P, C, D])
        wc1 = sb("wc1", [P, C, D])
        wmlp = sb("wmlp", [P, C * INNER + FT * D])
        wfc = wmlp[:, 0:C * INNER].rearrange("p (c n) -> p c n", c=C)
        wpj = wmlp[:, C * INNER:].rearrange("p (f n) -> p f n", f=FT)
        mk = wmlp[:, 0:B * QT * LK].rearrange("p (t k) -> p t k", k=LK)
        col = sb("col", [P, NCOL])
        row = sb("row", [P, len(ROW), D])
        ident = sb("ident", [P, P])
        identb = sb("identb", [P, P], BF16)
        colq = sb("colq", [P, 2, C])
        c0 = sb("c0", [P, 2, D])
        halfm = sb("halfm", [P, QT])
        ones = sb("ones", [P, LK], BF16)
        zeros = sb("zeros", [P, LQ], BF16)
        mkp = sb("mkp", [P, B, 3, QT, LK], BF16)
        mabs = sb("mabs", [P, 1])
        flag = sb("flag", [1, 1])
        kmrow8 = sb("kmrow8", [B, LK], U8)
        kmrow = sb("kmrow", [B, LK], BF16)
        kmcol8 = sb("kmcol8", [P, B * KT], U8)
        kmcol = sb("kmcol", [P, B * KT])
        cxT = sb("cxT", [P, C, LK])
        xTs = sb("xTs", [P, C, LQ])
        xs = sb("xs", [P, QT, D])
        xr = xs
        pf = sb("pf", [P, 2, LK])
        parts = sb("parts", [P, 2, 3, LK], BF16)
        ks0 = sb("ks0", [P, NG[0], LK], BF16)
        qs0 = sb("qs0", [P, NH[0], LQ], BF16)
        ks1 = sb("ks1", [P, 2, UH, LK], BF16)
        qs1 = sb("qs1", [P, 2, UH, LQ], BF16)
        vs = (sb("vs0", [P, B, KT, NG[0], HD[0] + 1]), sb("vs1", [P, B, KT, NG[1], HD[1] + 1]))
        mx = sb("mx", [P, 2, 2 * UH])
        mres = sb("mres", [2 * UH, 2, P])
        mparts = sb("mparts", [2 * UH, 2, 3, P], BF16)
        pt = sb("pt", [P, 3, BANKS, LK])
        oT = sb("oT", [P, 2, LK])
        rec = sb("rec", [P, 2, 2, QT, 4])
        att = sb("att", [P, QT, D])
        fT = sb("fT", [P, C, LQ])
        h0 = sb("h0", [P, QT, D])
        z = sb("z", [P, QT, D])
        x1 = h0
        res = sb("res", [P, B, QT, D])
        h1 = h0
        st6 = sb("st6", [P, QT, 6])
        mv = sb("mv", [P, 3, QT, 2])
        ve = sb("ve", [P, 3, QT])
        rstd = sb("rstd", [P, 3, QT])
        g = sb("g", [P, FT, LQ])
        bvb = g[:, 0:2, :].rearrange("p l (c m) -> p l c m", c=C)
        y = z

        sc = [ctx.enter_context(nc.psum_tensor(f"sc{i}", [P, LK], F32)) for i in range(2)]
        stb = [ctx.enter_context(nc.psum_tensor(f"st{i}", [P, LK], F32)) for i in range(3)]
        outp = ctx.enter_context(nc.psum_tensor("outp", [P, LK], F32))
        misc = [ctx.enter_context(nc.psum_tensor(f"misc{i}", [P, LK], F32)) for i in range(2)]

        D_ROWS = (PROD[0], MASK_ROW + 1)
        kd = tuple(nc.dram_tensor(f"kd{l}", [B, D_ROWS[l], NG[l], LK], BF16).ap() for l in range(2))
        qd = tuple(nc.dram_tensor(f"qd{l}", [B, D_ROWS[l], NH[l], LQ], BF16).ap() for l in range(2))

        WIDE = UH * LK + UH * LQ
        spare = mkp[:].rearrange("p b s t k -> p (b s t k)")

        def stack_slot(n):
            layer, _, u = UNITS[n]
            return u if layer == 0 else NU[0] + (n - C0) % CS

        def stack_use(n):
            layer, b, _ = UNITS[n]
            return b if layer == 0 else (n - C0) // CS

        def queries_of(n):
            layer, _, u = UNITS[n]
            if layer == 0:
                return qs0[:, u * UH:(u + 1) * UH, :]
            s = (n - C0) % CS
            if s < 2:
                return qs1[:, s]
            o = (s - 2) * WIDE + UH * LK
            return spare[:, o:o + UH * LQ].rearrange("p (h t) -> p h t", h=UH)

        def keys_of(n):
            layer, _, u = UNITS[n]
            if layer == 0:
                w = UH * NG[0] // NH[0]
                return ks0[:, u * w:(u + 1) * w, :]
            s = (n - C0) % CS
            if s < 2:
                return ks1[:, s]
            o = (s - 2) * WIDE
            return spare[:, o:o + UH * LK].rearrange("p (h t) -> p h t", h=UH)

        W_COUNT = (4, 2, 3, 1, 2)
        s_w = [sem(f"weights_in{i}") for i in range(len(W_COUNT))]
        s_mask = sem("mask_in")
        s_km = sem("keymask_in")
        s_pinit = sem("pool_setup_step")
        s_kmr = sem("keymask_row_ready")
        s_dinit = sem("dve_setup_done")
        s_const = sem("consts_ready")
        s_fl = sem("mask_magnitude_ready")
        s_mks = sem("mask_split_step")
        s_mkp = sem("mask_parts")
        s_ctx = sem("ctx_in")
        s_xT = sem("xT_in")
        s_x = sem("x_in")
        s_xr = sem("xr_ready")
        s_mf = [sem(f"misc_full{i}") for i in range(2)]
        s_me = [sem(f"misc_read{i}") for i in range(2)]
        s_pt = sem("parts_ready")
        s_pool = sem("pool_step")
        s_dve = sem("dve_step")
        s_wr = [sem(f"parts_written{i}") for i in range(2)]
        s_rows = sem("constant_rows_written")
        s_st = [sem(f"stack_in{i}") for i in range(NU[0] + CS)]
        s_sf = sem("scores_full")
        s_sr = sem("scores_reduced")
        s_tf = sem("shifted_full")
        s_ex = sem("exp_done")
        s_pv = sem("pv_done")
        s_oe = sem("out_evacuated")
        s_mp = sem("max_parts_ready")
        s_mi = [sem(f"max_in{i}") for i in range(2)]
        s_mv = sem("moments_ready")
        s_rs = sem("rstd_ready")
        s_z = sem("normed_ready")
        s_x1 = sem("x1_ready")
        s_x1r = sem("x1_biased")
        s_h1r = sem("h1_biased")
        s_out = sem("out_written")

        def full(eng, n, b):
            bank, i = PLACE[n, b]
            eng.wait_ge(s_mf[bank], i + 1)
            return misc[bank]

        def take(eng, n, b):
            bank, i = PLACE[n, b]
            if i > 0:
                eng.wait_ge(s_me[bank], i)
            return misc[bank]

        def filled(ins, n, b):
            ins.then_inc(s_mf[PLACE[n, b][0]], 1)

        def freed(ins, n, b):
            return ins.then_inc(s_me[PLACE[n, b][0]], 1)

        def emptied(eng, b, *names):
            for n in names:
                bank, i = PLACE[n, b]
                eng.wait_ge(s_me[bank], i + 1)

        class Chain:
            def __init__(self, s):
                self.s, self.k = s, 0

            def link(self, eng, ins):
                ins.then_inc(self.s, 1)
                self.k += 1
                eng.wait_ge(self.s, self.k)

        def await_(eng, s, value):
            if value > 0:
                eng.wait_ge(s, value)

        WR = PAIRS * 16
        NORM = {(0, b): None for b in range(B)}
        norms = sorted([(AT["w0", b], 0, b) for b in range(B)] + [(AT["w0", b] + 1, 1, b) for b in range(B)]
                       + [(AT["w1", b], 2, b) for b in range(B)])
        NORM = {(i, b): k for k, (_, i, b) in enumerate(norms)}
        ZS = {nb: k for k, nb in enumerate([(n, b) for _, n, b in OPS if n in ("y1", "y2")])}

        def c1(n, c=0, rows=P):
            k = COL[n][0] + c
            return col[0:rows, k:k + 1]

        block = ctx.enter_context(nc.Block())

        @block.sync
        def _(sp):
            def load_ctx(b):
                sp.dma_start(cxT[:], ctxT[b:b + 1].rearrange("o (c p) k -> p (o c) k", p=P)).then_inc(s_ctx, 16)

            def load_xT(b):
                sp.dma_start(xTs[:], xT[b:b + 1].rearrange("o (c p) q -> p (o c) q", p=P)).then_inc(s_xT, 16)

            def load_x(b):
                sp.dma_start(xs[:], x[b:b + 1].rearrange("o (t p) d -> p (o t) d", p=P)).then_inc(s_x, 16)

            def write(i):
                _, n, b, c = SPLITS[i]
                layer = int(n[1])
                d = HD[layer]
                if n[0] == "k":
                    dst, part_of, width = kd[layer], K_PART, LK
                    h0_, nh = (0, NG[0]) if layer == 0 else (int(n[-1]) * 8, 8)
                else:
                    dst, part_of, width = qd[layer], Q_PART, LQ
                    nh = P // d
                    h0_ = c * nh
                sp.wait_ge(s_pt, i + 1)
                for k in range(PAIRS):
                    to = dst[b:b + 1, k * d:(k + 1) * d, h0_:h0_ + nh, :].rearrange("o d h t -> (o h) d t")
                    sp.dma_start(to, parts[0:nh * d, i % 2, part_of[k], 0:width]).then_inc(s_wr[i % 2], 16)

            def written(*names):
                for key in names:
                    i = SPLIT[key]
                    sp.wait_ge(s_wr[i % 2], (i // 2 + 1) * WR)

            def read(n):
                layer, b, u = UNITS[n]
                R = D_ROWS[layer]
                if layer == 0:
                    written(("k0", b, 0), ("q0", b, u * C // NU[0]))
                    if b > 0:
                        sp.wait_ge(s_tf, (n - NU[0] + 1) * STEPS * BANKS)
                    else:
                        sp.wait_ge(s_dinit, 1)
                        sp.wait_ge(s_pinit, 3)
                    w = UH * NG[0] // NH[0]
                else:
                    if n == C0:
                        sp.wait_ge(s_rows, 64)
                    written((f"k1_{u}", b, 0), ("q1", b, u))
                    c = n - C0
                    if c >= CS:
                        sp.wait_ge(s_tf, (n - CS + 1) * STEPS * BANKS)
                    elif c >= 2:
                        sp.wait_ge(s_mkp, (c - 1) * (B // 2))
                        sp.wait_ge(s_tf, (c - 1) * (B // 2) * AS * BANKS)
                    w = UH
                s = s_st[stack_slot(n)]
                sp.dma_start(keys_of(n)[0:R], kd[layer][b:b + 1, 0:R, u * w:(u + 1) * w, :]
                             .rearrange("o r h t -> (o r) h t")).then_inc(s, 16)
                sp.dma_start(queries_of(n)[0:R], qd[layer][b:b + 1, 0:R, u * UH:(u + 1) * UH, :]
                             .rearrange("o r h t -> (o r) h t")).then_inc(s, 16)

            def max_rows(n):
                sp.wait_ge(s_mp, n + 1)
                if UNITS[n][0] == 1:
                    sp.wait_ge(s_sf, (n + 1) * STEPS * BANKS)
                for i in range(3):
                    r = M_ROW + i
                    sp.dma_start(queries_of(n)[r:r + 1], mparts[:, n % 2, i, :]).then_inc(s_mi[n % 2], 16)

            def constant_rows():
                n1 = 3 * NG[1]
                sp.wait_ge(s_dinit, 1)
                sp.wait_ge(s_kmr, 1)
                sp.dma_start(kd[1][:, M_ROW:MASK_ROW].rearrange("b r h t -> (r h) b t"),
                             ones[0:n1].unsqueeze(1).to_broadcast([n1, B, LK])).then_inc(s_rows, 16)
                sp.dma_start(kd[1][:, MASK_ROW:MASK_ROW + 1].rearrange("b r h t -> b (r h) t"),
                             kmrow[:].unsqueeze(1).to_broadcast([B, NG[1], LK])).then_inc(s_rows, 16)
                sp.dma_start(qd[1][:, M_ROW:MASK_ROW].rearrange("b r h t -> (r h) b t"),
                             zeros[0:n1].unsqueeze(1).to_broadcast([n1, B, LQ])).then_inc(s_rows, 16)
                sp.dma_start(qd[1][:, MASK_ROW:MASK_ROW + 1].rearrange("b r h t -> (r h) b t"),
                             ones[0:NH[1], 0:LQ].unsqueeze(1).to_broadcast([NH[1], B, LQ])).then_inc(s_rows, 16)

            def read_at(n):
                layer, b, u = UNITS[n]
                if layer == 0:
                    return -1 if b == 0 else (n - NU[0] + 1) * STEPS + LAG
                c = n - C0
                free = ((n - CS + 1) * STEPS if c >= CS else (c - 1) * (B // 2) * AS if c >= 2 else 0) + LAG
                return max(free, AT["q1", b] + 4 + 2 * u)

            load_ctx(0)
            load_xT(0)
            sp.dma_start(mk, mask.rearrange("b (t p) k -> p (b t) k", p=P)).then_inc(s_mask, 16)
            load_x(0)
            for t in range(-1, END + 1):
                if t > 0 and t % STEPS == 0 and t // STEPS <= len(UNITS):
                    max_rows(t // STEPS - 1)
                late = 0 if t < 0 else 2
                for i, (at, _, _, _) in enumerate(SPLITS):
                    if at == -1 and t == -1 or at >= 0 and at + 2 == t:
                        write(i)
                for n in range(len(UNITS)):
                    if read_at(n) == t:
                        read(n)
                for n, b in ops_at(t - 1):
                    if n == "k1_1" and b < B - 1:
                        full(sp, n, b)
                        load_ctx(b + 1)
                        load_xT(b + 1)
                    if n == "w0" and b < B - 1:
                        emptied(sp, b, n)
                        load_x(b + 1)
                    if n == "p1":
                        emptied(sp, b, n)
                        sp.dma_start(out[b:b + 1].rearrange("o (t p) d -> p (o t) d", p=P), y[:]).then_inc(s_out, 16)
                if t == AS - 2:
                    sp.wait_ge(s_mkp, B)
                    sp.dma_start(wfc, fcw.rearrange("(c p) n -> p c n", p=P)).then_inc(s_w[4], 16)
                    sp.dma_start(wpj, pjw.rearrange("(c p) n -> p c n", p=P)).then_inc(s_w[4], 16)
                    constant_rows()
            sp.wait_ge(s_out, 16 * B)

        @block.gpsimd
        def _(pool):
            chain = Chain(s_pool)
            setup = Chain(s_pinit)
            setup.link(pool, pool.memset(halfm[:], -0.5))
            setup.link(pool, pool.memset(ks0[0:M_ROW], 0.0))
            setup.link(pool, pool.memset(ks0[M_ROW:M_ROW + 3], 1.0))
            for l in range(2):
                setup.link(pool, pool.memset(vs[l][:].rearrange("p b t h d -> p (b t h) d")[:, :, HD[l]:HD[l] + 1], 1.0))
            pool.wait_ge(s_w[0], 16 * W_COUNT[0])
            for l, n in enumerate(("bq0", "bq1")):
                k = COL[n][0]
                last = pool.tensor_scalar(colq[:, l, :], col[:, k:k + C], SCALE[l], None, ALU.mult)
            last.then_inc(s_const, 1)

            def masks():
                pool.wait_ge(s_km, 32)
                setup.link(pool, pool.tensor_scalar(kmcol[:], kmcol8[:], FAR, -FAR, ALU.mult, ALU.add))
                pool.tensor_scalar(kmrow[:], kmrow8[:], FAR, -FAR, ALU.mult,
                                   ALU.add).then_inc(s_kmr, 1)
                pool.wait_ge(s_kmr, 1)

            def biases():
                for l, n in enumerate(("bv0", "bv1")):
                    for c in range(C):
                        last = pool.tensor_copy(bvb[:, l, c, :], c1(n, c).to_broadcast([P, P]))
                last.then_inc(s_const, 1)

            def split(i):
                _, name, b, _ = SPLITS[i]
                s = i % 2
                r = KF[0] if name == "k0" else P
                n = LK if name[0] == "k" else LQ
                emptied(pool, b, name)
                await_(pool, s_wr[s], i // 2 * WR)
                a, p3 = pf[0:r, s, 0:n], parts[0:r, s, :, 0:n]
                chain.link(pool, pool.tensor_copy(p3[:, 0], a))
                chain.link(pool, pool.tensor_tensor(a, a, p3[:, 0], ALU.subtract))
                chain.link(pool, pool.tensor_copy(p3[:, 1], a))
                pool.tensor_tensor(p3[:, 2], a, p3[:, 1], ALU.subtract).then_inc(s_pt, 1)

            def inv_std(b, i):
                pool.wait_ge(s_mv, NORM[i, b] + 1)
                chain.link(pool, pool.tensor_scalar(ve[:, i, :], mv[:, i, :, 1], EPS[i], None, ALU.add))
                pool.tensor_tensor(rstd[:, i, :], ve[:, i, :], halfm[:], ALU.pow).then_inc(s_rs, 1)

            def split_mask(b):
                m, p3 = mk[:, b * QT:(b + 1) * QT, :], mkp[:, b]
                if b == 0:
                    pool.wait_ge(s_mask, 16)
                    pool.wait_ge(s_fl, 1)
                steps = Chain(s_mks)
                steps.k = 4 * b
                steps.link(pool, pool.tensor_scalar(m, m, -FAR, FAR, ALU.max, ALU.min))
                steps.link(pool, pool.tensor_copy(p3[:, 0], m))
                steps.link(pool, pool.tensor_tensor(m, m, p3[:, 0], ALU.subtract))
                steps.link(pool, pool.tensor_copy(p3[:, 1], m))
                pool.tensor_tensor(p3[:, 2], m, p3[:, 1], ALU.subtract).then_inc(s_mkp, 1)

            for t in range(-1, END):
                for n, b in ops_at(t):
                    if n == "w0":
                        inv_std(b, 0)
                    if n == "w1":
                        inv_std(b, 2)
                        emptied(pool, b, "w1")
                        pool.tensor_tensor(res[:, b], h1[:], row[:, ROW["pb"]:ROW["pb"] + 1, :].to_broadcast([P, QT, D]),
                                           ALU.add).then_inc(s_h1r, 1)
                for n, b in ops_at(t - 1, ("w0",)):
                    inv_std(b, 1)
                    pool.wait_ge(s_x1, b + 1)
                    pool.tensor_tensor(res[:, b], x1[:], c0[:, 1:2, :].to_broadcast([P, QT, D]),
                                       ALU.add).then_inc(s_x1r, 1)
                for i, (at, _, _, _) in enumerate(SPLITS):
                    if at == t:
                        split(i)
                if t == -1:
                    split_mask(0)
                if t == 0:
                    biases()
                    pool.tensor_copy(identb[:], ident[:]).then_inc(s_const, 1)
                if t == 3:
                    masks()
                if t % AS == AS - 2 and t < C0 * STEPS:
                    b = t // AS
                    emptied(pool, 0, "c0")
                    pool.wait_ge(s_x, 16 * (b + 1))
                    pool.tensor_tensor(xr[:], xs[:], c0[:, 0:1, :].to_broadcast([P, QT, D]), ALU.add).then_inc(s_xr, 1)
                if t in (6, 9, 12):
                    split_mask(t // 3 - 1)

        @block.vector
        def _(dve):
            chain = Chain(s_dve)
            dve.memset(ones[:], 1.0)
            dve.memset(zeros[:], 0.0)
            dve.memset(outp[:], 0.0)
            dve.memset(qs0[0:M_ROW], 0.0).then_inc(s_dinit, 1)

            def values(b, t):
                m = full(dve, f"v{t}", b)
                dve.tensor_copy(vs[0][:, b, t, :, 0:HD[0]], m[:, 0:KF[0]].rearrange("p (g d) -> p g d", d=HD[0]))
                ins = dve.tensor_copy(vs[1][:, b, t, :, 0:HD[1]],
                                      m[:, KF[0]:KF[0] + KF[1]].rearrange("p (g d) -> p g d", d=HD[1]))
                freed(ins, f"v{t}", b)

            def find_mask():
                dve.wait_ge(s_mask, 16)
                dve.tensor_reduce(mabs[:], mk, AX.XY, ALU.max, apply_absolute_value=True).then_inc(s_fl, 1)
                m = full(dve, "flag", 0)
                freed(dve.tensor_reduce(flag[:], m[0:1, 0:P], AX.X, ALU.max), "flag", 0)

            def biases():
                m = full(dve, "c0", 0)
                for l, n in enumerate(("bo", "cb")):
                    ins = dve.tensor_tensor(c0[:, l, :], m[:, l * D:(l + 1) * D], row[:, ROW[n], :], ALU.add)
                freed(ins, "c0", 0)

            def maxima(s):
                n = s // STEPS
                for i in range(BANKS):
                    k = s * BANKS + i
                    dve.wait_ge(s_sf, k + 1)
                    c = k % (2 * UH)
                    dve.tensor_reduce(mx[:, n % 2, c:c + 1], sc[k % 2][:], AX.X, ALU.max,
                                      negate=True).then_inc(s_sr, 1)

            def split_maxima(n):
                m = full(dve, "m", n)[0:2 * UH, 0:P]
                s = n % 2
                await_(dve, s_mi[s], n // 2 * 48)
                chain.link(dve, dve.tensor_copy(mparts[:, s, 0, :], m))
                freed(dve.tensor_tensor(mres[:, s, :], m, mparts[:, s, 0, :], ALU.subtract), "m", n)
                emptied(dve, n, "m")
                chain.link(dve, dve.tensor_copy(mparts[:, s, 1, :], mres[:, s, :]))
                dve.tensor_tensor(mparts[:, s, 2, :], mres[:, s, :], mparts[:, s, 1, :],
                                  ALU.subtract).then_inc(s_mp, 1)

            def normalise(n):
                layer, b, u = UNITS[n]
                d = HD[layer]
                m = full(dve, "o", n)
                v = m[:].rearrange("p (h t j w) -> p h t j w", h=2, t=QT, w=VW)
                r = rec[:, n % 2]
                chain.link(dve, dve.reciprocal(r.rearrange("p h t j -> p (h t) j"),
                                               m[:].rearrange("p (a j w) -> p a j w", a=2 * QT, w=VW)[:, :, :, d]))
                if u == 0 and n > 0:
                    full(dve, f"a{UNITS[n - 1][0]}", UNITS[n - 1][1])
                a = att[:, :, u * UH * d:(u + 1) * UH * d].rearrange("p t (j h d) -> p h t j d", h=2, d=d)
                for h in range(2):
                    ins = dve.tensor_tensor(a[:, h], v[:, h, :, :, 0:d],
                                            r[:, h].unsqueeze(3).to_broadcast([P, QT, 4, d]), ALU.mult)
                freed(ins, "o", n)

            def moments(b, i, src):
                for t in range(QT):
                    ins = dve.bn_stats(st6[:, t, :], src[:, t, :])
                chain.link(dve, ins)
                for t in range(QT):
                    ins = dve.bn_aggr(mv[:, i, t, :], st6[:, t, :])
                ins.then_inc(s_mv, 1)

            def centre(b, i, src):
                dve.wait_ge(s_rs, NORM[i, b] + 1)
                for t in range(QT):
                    ins = dve.tensor_scalar(z[:, t, :], src[:, t, :], mv[:, i, t, 0:1], rstd[:, i, t:t + 1],
                                            ALU.subtract, ALU.mult)
                return ins

            def flat(a):
                return a.rearrange("p t d -> p (t d)")

            def rowb(n):
                return row[:, ROW[n]:ROW[n] + 1, :].to_broadcast([P, QT, D])

            for t in range(-1, END):
                if 0 <= t < ALL:
                    maxima(t)
                for n, b in ops_at(t):
                    if n[0] == "v":
                        values(b, int(n[1]))
                    if n == "flag":
                        find_mask()
                    if n == "c0":
                        biases()
                    if n == "m":
                        split_maxima(b)
                    if n == "o":
                        normalise(b)
                    if n == "w0":
                        m = full(dve, n, b)
                        dve.wait_ge(s_xr, b + 1)
                        await_(dve, s_x1r, b)
                        freed(dve.tensor_tensor(flat(h0[:]), m[:], flat(xr[:]), ALU.add), n, b)
                        emptied(dve, b, n)
                        moments(b, 0, h0)
                    if n == "w1":
                        m = full(dve, n, b)
                        dve.wait_ge(s_x1r, B)
                        await_(dve, s_h1r, b)
                        freed(dve.tensor_tensor(flat(h1[:]), m[:], flat(res[:, b]), ALU.add), n, b)
                        emptied(dve, b, n)
                        moments(b, 2, h1)
                    if n[0] == "p":
                        m = full(dve, n, b)
                        q = int(n[1])
                        dve.wait_ge(s_h1r, b + 1)
                        freed(dve.tensor_tensor(y[:, q, :], m[:, 0:D], res[:, b, q, :], ALU.add), n, b)
                for n, b in ops_at(t - 1):
                    if n == "w0":
                        if b > 0:
                            full(dve, "y1", b - 1)
                        chain.link(dve, centre(b, 0, h0))
                        chain.link(dve, dve.tensor_tensor(h0[:], z[:], rowb("gamma"), ALU.mult))
                        dve.tensor_tensor(x1[:], h0[:], rowb("beta"), ALU.add).then_inc(s_x1, 1)
                        dve.wait_ge(s_x1, b + 1)
                        moments(b, 1, x1)
                    if n == "w1":
                        full(dve, "y2" if b else "y1", b - 1 if b else B - 1)
                        await_(dve, s_out, 16 * b)
                        centre(b, 2, h1).then_inc(s_z, 1)
                for n, b in ops_at(t - 2, ("w0",)):
                    centre(b, 1, x1).then_inc(s_z, 1)

        @block.scalar
        def _(act):
            def load(i, tile, src):
                act.dma_start(tile[:], src).then_inc(s_w[i], 16)

            load(0, col, cols)
            load(0, wk0, Wk0.rearrange("(c p) n -> p c n", p=P))
            load(0, wq0, Wq0.rearrange("(c p) n -> p c n", p=P))
            load(0, ident, eye)
            load(1, wv, Wv.rearrange("(c p) n -> p c n", p=P))
            load(1, wk1, Wk1.rearrange("(c p) n -> p c n", p=P))
            act.dma_start(kmcol8[:], keymaskT).then_inc(s_km, 16)
            act.dma_start(kmrow8[:], keymask).then_inc(s_km, 16)
            load(2, wo0, Wo0.rearrange("(c p) n -> p c n", p=P))
            load(2, wc1, Wc1.rearrange("(c p) n -> p c n", p=P))
            load(2, row, rows.to_broadcast([P, len(ROW), D]))
            load(3, wq1, Wq1.rearrange("(c p) n -> p c n", p=P))

            def exps(s):
                layer, b, _ = UNITS[s // STEPS]
                kt = s % STEPS
                for j in range(BANKS):
                    k = s * BANKS + j
                    act.wait_ge(s_tf, k + 1)
                    if j == 0:
                        await_(act, s_pv, s - 2)
                    bias = kmcol[:, b * KT + kt:b * KT + kt + 1] if layer else 0.0
                    act.activation(pt[:, s % 3, j, :], stb[k % 3][:], ACT.Exp, bias=bias).then_inc(s_ex, 1)

            def evacuate(n):
                act.wait_ge(s_pv, (n + 1) * STEPS)
                if n > 1:
                    full(act, "o", n - 2)
                act.copy(oT[:, n % 2, :], outp[:]).then_inc(s_oe, 1)

            def project(name, b):
                m = full(act, name, b)
                for c in range(2 if name[0] == "q" else 1):
                    i = SPLIT[name, b, c]
                    await_(act, s_pt, i - 1)
                    if name[0] == "q":
                        l = int(name[1])
                        ins = act.activation(pf[:, i % 2, 0:LQ], m[:, c * LQ:(c + 1) * LQ], ACT.Identity,
                                             bias=colq[:, l, c:c + 1], scale=SCALE[l])
                    elif name == "k0":
                        ins = act.activation(pf[0:KF[0], i % 2, :], m[0:KF[0], :], ACT.Identity, bias=c1("bk0", rows=KF[0]))
                    else:
                        ins = act.activation(pf[:, i % 2, :], m[:], ACT.Identity, bias=c1("bk1", int(name[-1])))
                freed(ins, name, b)

            def norm_affine(n, b, ln):
                m = full(act, n, b)
                for c in range(C):
                    ins = act.activation(fT[:, c, :], m[:, c * LQ:(c + 1) * LQ], ACT.Identity, bias=c1(ln + "b", c),
                                         scale=c1(ln + "w", c))
                freed(ins, n, b)

            act.wait_ge(s_const, 1)
            for t in range(-1, END):
                if t == C0 * STEPS + LAG:
                    act.wait_ge(s_kmr, 1)
                if 0 <= t - LAG < ALL:
                    exps(t - LAG)
                n = (t - LAG) // STEPS - 1
                if t % STEPS == (LAG + STEPS) % STEPS and 0 <= n < len(UNITS):
                    evacuate(n)
                for n, b in ops_at(t):
                    if (n, b, 0) in SPLIT:
                        project(n, b)
                    if n in ("a0", "a1"):
                        m = full(act, n, b)
                        freed(act.copy(fT[:].rearrange("p c q -> p (c q)"), m[:]), n, b)
                    if n == "y1":
                        norm_affine(n, b, "ln1")
                    if n == "y2":
                        norm_affine(n, b, "ln2")
                    if n[0] == "f" and n != "flag":
                        m = full(act, n, b)
                        i = int(n[1])
                        for k in range(2):
                            ins = act.activation(g[:, 2 * i + k, :], m[:, k * LQ:(k + 1) * LQ], ACT.Gelu_apprx_tanh,
                                                 bias=c1("fcb", 2 * i + k))
                        freed(ins, n, b)

        @block.tensor
        def _(pe):
            def product(out_, pairs):
                for i, (l, r) in enumerate(pairs):
                    ins = pe.matmul(out_, l, r, start=i == 0, stop=i == len(pairs) - 1)
                return ins

            def scores(s, i, add_mask):
                n = s // STEPS
                layer, b, u = UNITS[n]
                if s % STEPS == 0 and i == 0:
                    pe.wait_ge(s_st[stack_slot(n)], 32 * (stack_use(n) + 1))
                k = s * BANKS + i
                h, t = k % (2 * UH) // QT, k % QT
                await_(pe, s_sr, k - 1)
                more = add_mask and layer == 0
                R = S_ROWS[layer]
                ins = pe.matmul(sc[k % 2][:], queries_of(n)[0:R, h, t * P:(t + 1) * P],
                                keys_of(n)[0:R, h * NG[layer] // NH[layer], :], start=True, stop=not more)
                if more:
                    for p in range(3):
                        ins = pe.matmul(sc[k % 2][:], identb[:], mkp[:, b, p, t, :], start=False, stop=p == 2)
                ins.then_inc(s_sf, 1)

            def shifted(s, j, add_mask):
                n, kt = s // STEPS, s % STEPS
                layer, b, u = UNITS[n]
                if kt == 0 and j == 0:
                    pe.wait_ge(s_mi[n % 2], (n // 2 + 1) * 48)
                k = s * BANKS + j
                bank = stb[k % 3]
                await_(pe, s_ex, k - 2)
                more = add_mask and layer == 0
                R = ST_ROWS
                hs = 2 if layer == 0 else 1
                for i in range(0, 2, hs):
                    h = 2 * j + i
                    ins = pe.matmul(bank[:, i * LQ:(i + hs) * LQ],
                                    keys_of(n)[0:R, h * NG[layer] // NH[layer], kt * P:(kt + 1) * P],
                                    queries_of(n)[0:R, h:h + hs, :], start=True, stop=not more)
                if more:
                    o = bank[:].rearrange("p (h t q) -> p h t q", h=2, q=P)
                    for p in range(3):
                        for t in range(QT):
                            ins = pe.matmul(o[:, :, t, :], mkp[:, b, p, t, kt * P:(kt + 1) * P],
                                            identb[:].unsqueeze(1).to_broadcast([P, 2, P]),
                                            start=False, stop=p == 2 and t == QT - 1)
                ins.then_inc(s_tf, 1)

            def values(s):
                n, kt = s // STEPS, s % STEPS
                layer, b, u = UNITS[n]
                w = HD[layer] + 1
                if n == 0 and kt == 0:
                    pe.wait_ge(s_dinit, 1)
                if kt == 0:
                    await_(pe, s_oe, n)
                    if u == 0 and layer == 0:
                        emptied(pe, b, *(f"v{t}" for t in range(KT)))
                pe.wait_ge(s_ex, (s + 1) * BANKS)
                for j in range(BANKS):
                    to = outp[VW * j:VW * j + w, :]
                    if layer == 0:
                        gs = (u * UH + 2 * j) * NG[0] // NH[0]
                        ins = pe.matmul(to, vs[0][:, b, kt, gs, :], pt[:, s % 3, j, :], start=kt == 0, stop=kt == KT - 1)
                    else:
                        for i in range(2):
                            ins = pe.matmul(to[:, i * LQ:(i + 1) * LQ], vs[1][:, b, kt, u * UH + 2 * j + i, :],
                                            pt[:, s % 3, j, i * LQ:(i + 1) * LQ],
                                            start=kt == 0 and i == 0, stop=kt == KT - 1, skip_group_check=True)
                ins.then_inc(s_pv, 1)

            def turn(m, src):
                for c in range(C):
                    for t in range(QT):
                        ins = pe.transpose(m[:, c * LQ + t * P:c * LQ + (t + 1) * P], src[:, t, c * P:(c + 1) * P], ident[:])
                return ins

            def to_model(m, w):
                for t in range(QT):
                    ins = product(m[:, t * D:(t + 1) * D], [(fT[:, c, t * P:(t + 1) * P], w[:, c, :]) for c in range(C)])
                return ins

            def queries(m, w, src):
                for o in range(C):
                    ins = product(m[:, o * LQ:(o + 1) * LQ], [(w[:, c, o * P:(o + 1) * P], src[:, c, :]) for c in range(C)])
                return ins

            def dense(n, b):
                m = take(pe, n, b)
                if n == "k0":
                    if b == 0:
                        pe.wait_ge(s_w[0], 16 * W_COUNT[0])
                    pe.wait_ge(s_ctx, 16 * (b + 1))
                    ins = product(m[0:KF[0], :], [(wk0[:, c, :], cxT[:, c, :]) for c in range(C)])
                elif n == "q0":
                    pe.wait_ge(s_xT, 16 * (b + 1))
                    ins = queries(m, wq0, xTs)
                elif n[0] == "v":
                    if b == 0:
                        pe.wait_ge(s_w[1], 16 * W_COUNT[1])
                    t = int(n[1])
                    ins = product(m[:, 0:KF[0] + KF[1]], [(cxT[:, c, t * P:(t + 1) * P], wv[:, c, :]) for c in range(C)])
                elif n[:2] == "k1":
                    o = int(n[-1])
                    ins = product(m[:], [(wk1[:, c, o * P:(o + 1) * P], cxT[:, c, :]) for c in range(C)])
                elif n == "flag":
                    pe.wait_ge(s_fl, 1)
                    ins = pe.transpose(m[0:1, 0:P], mabs[:], ident[:])
                elif n == "c0":
                    pe.wait_ge(s_const, 2)
                    pe.wait_ge(s_w[2], 16 * W_COUNT[2])
                    for l, w in enumerate((wo0, wc1)):
                        ins = product(m[:, l * D:(l + 1) * D], [(bvb[:, l, c, :], w[:, c, :]) for c in range(C)])
                elif n == "m":
                    pe.wait_ge(s_sr, (b + 1) * STEPS * BANKS)
                    ins = pe.transpose(m[0:2 * UH, 0:P], mx[:, b % 2, :], ident[:])
                elif n == "o":
                    pe.wait_ge(s_oe, b + 1)
                    for i in range(2 * QT):
                        ins = pe.transpose(m[:, i * P:(i + 1) * P], oT[:, b % 2, i * P:(i + 1) * P], ident[:])
                elif n in ("a0", "a1"):
                    layer = int(n[1])
                    first = b * NU[layer] + layer * C0
                    for k in range(NU[layer]):
                        emptied(pe, first + k, "o")
                    ins = turn(m, att)
                elif n == "w0":
                    emptied(pe, b, "a0")
                    ins = to_model(m, wo0)
                elif n == "w1":
                    emptied(pe, b, "a1")
                    ins = to_model(m, wc1)
                elif n in ("y1", "y2"):
                    pe.wait_ge(s_z, ZS[n, b] + 1)
                    ins = turn(m, z)
                elif n == "q1":
                    if b == 0:
                        pe.wait_ge(s_w[3], 16 * W_COUNT[3])
                    emptied(pe, b, "y1")
                    ins = queries(m, wq1, fT)
                elif n[0] == "f":
                    if b == 0:
                        pe.wait_ge(s_w[4], 16 * W_COUNT[4])
                    emptied(pe, b, "y2")
                    i = int(n[1])
                    for k in range(2):
                        o = 2 * i + k
                        ins = product(m[:, k * LQ:(k + 1) * LQ], [(wfc[:, c, o * P:(o + 1) * P], fT[:, c, :]) for c in range(C)])
                else:
                    t = int(n[1])
                    emptied(pe, b, *(f"f{i}" for i in range(FT // 2)))
                    ins = product(m[:, 0:D], [(g[:, f, t * P:(t + 1) * P], wpj[:, f, :]) for f in range(FT)])
                filled(ins, n, b)

            def attention(add_mask):
                for t in range(END):
                    if add_mask and t % AS == 0 and t < C0 * STEPS:
                        pe.wait_ge(s_mkp, t // AS + 1)
                        pe.wait_ge(s_const, 3)
                    for i in range(BANKS):
                        if t < ALL:
                            scores(t, i, add_mask)
                        if 0 <= t - LAG < ALL:
                            shifted(t - LAG, i, add_mask)
                    if 0 <= t - LAG - 1 < ALL:
                        values(t - LAG - 1)
                    for n, b in ops_at(t):
                        dense(n, b)

            for n, b in ops_at(-1):
                dense(n, b)
            emptied(pe, 0, "flag")
            masked = pe.value_load(flag[0:1, 0:1].bitcast(I32))
            with pe.If(masked != 0):
                attention(True)
            with pe.Else():
                attention(False)


def kernel(**inputs):
    import concourse.bacc as _bacc
    from concourse.bass_utils import run_bass_kernel_spmd as _run

    a = {n: np.asarray(v) for n, v in inputs.items()}
    l0 = {n[len("L0_xattn_"):]: v for n, v in a.items() if n.startswith("L0_xattn_")}
    l1 = {n[len("L1_xattn_"):]: v for n, v in a.items() if n.startswith("L1_xattn_")}

    def columns(v):
        return v.reshape(-1, P).T

    bv0 = np.repeat(l0["bv"].reshape(NG[0], 1, HD[0]), NH[0] // NG[0], axis=1).reshape(D)
    bk0 = np.concatenate([l0["bk"], np.zeros(P - KF[0], np.float32)])
    vectors = {"bq0": l0["bq"], "bk0": bk0, "bv0": bv0, "bq1": l1["q_b"], "bk1": l1["k_b"], "bv1": l1["v_b"],
               "ln1w": l1["ln1_w"], "ln1b": l1["ln1_b"], "ln2w": l1["ln2_w"], "ln2b": l1["ln2_b"], "fcb": l1["fc_b"]}
    broad = {"bo": l0["bo"], "gamma": l0["gamma"], "beta": l0["beta"], "cb": l1["cproj_b"], "pb": l1["proj_b"]}
    keymask = a["mask_BxS2_bf1"].view(np.uint8)
    arrays = {
        "xT": a["x"].transpose(0, 2, 1),
        "x": a["x"],
        "ctxT": a["ctx_2048"].transpose(0, 2, 1),
        "mask": a["mask_Bx1xSxS2_ff0"].reshape(B, LQ, LK),
        "keymask": keymask.reshape(B, LK),
        "keymaskT": keymask.reshape(B * KT, P).T,
        "Wq0": l0["Wq"], "Wk0": l0["Wk"], "Wv": np.concatenate([l0["Wv"], l1["v_w"]], axis=1), "Wo0": l0["Wo"],
        "Wq1": l1["q_w"], "Wk1": l1["k_w"], "Wc1": l1["cproj_w"], "fcw": l1["fc_w"], "pjw": l1["proj_w"],
        "cols": np.concatenate([columns(vectors[n]) for n in COL], axis=1),
        "rows": np.stack([broad[n] for n in ROW])[None],
        "eye": np.eye(P, dtype=np.float32),
    }
    arrays = {n: np.ascontiguousarray(v) for n, v in arrays.items()}
    nc = _bacc.Bacc("TRN2", target_bir_lowering=False, num_devices=1)
    args = [nc.dram_tensor(f"in_{n}", v.shape, mybir.dt.from_np(v.dtype), kind="ExternalInput").ap()
            for n, v in arrays.items()]
    out = nc.dram_tensor("out", (B, LQ, D), F32, kind="ExternalOutput").ap()
    build(nc, *args, out)
    r = _run(nc, [{f"in_{n}": v for n, v in arrays.items()}], core_ids=[0])
    return r.results[0]["out"]
```

```python
from contextlib import ExitStack

import numpy as np

import concourse.bass as bass
from concourse import mybir

ALU = mybir.AluOpType
ACT = mybir.ActivationFunctionType
AX = mybir.AxisListType
F32 = mybir.dt.float32
BF16 = mybir.dt.bfloat16
I32 = mybir.dt.int32
U8 = mybir.dt.uint8

B, LQ, LK, D = 4, 256, 512, 256
P = 128
QT, KT, C = LQ // P, LK // P, D // P
INNER = 4 * D
FT = INNER // P
HD = (8, 16)
NH = (32, 16)
NG = (8, 16)
KF = tuple(g * d for g, d in zip(NG, HD))
UH = 8
NU = tuple(h // UH for h in NH)
STEPS = 4
BANKS = 4
SR, TR = 3, 2
LAG = 8
VW = 32
Q_PART = (0, 0, 0, 1, 1, 2)
K_PART = (0, 1, 2, 0, 1, 0)
PAIRS = len(Q_PART)
PROD = tuple(PAIRS * d for d in HD)
M_ROW = 96
MASK_ROW = M_ROW + 3
S_ROWS = (M_ROW, MASK_ROW + 1)
ST_ROWS = M_ROW + 3
CS = 4
SCALE = tuple(float(d) ** -0.5 for d in HD)
FAR = float(2.0 ** 127)
EPS = (1e-6, 1e-5, 1e-5)

UNITS = [(0, b, u) for b in range(B) for u in range(NU[0])] + [(1, b, u) for b in range(B) for u in range(NU[1])]
L1_FIRST = B * NU[0]
BATCH_STEPS = NU[0] * STEPS
ALL = len(UNITS) * STEPS


LB = LAG * BANKS
NEW = {"k0": 10, "q0": 19, "v0": 19, "v1": 20, "v2": 20, "v3": 26, "k1_0": 54, "k1_1": 66}
SECOND = 4
BIAS_AT = 37
WHEN = {"m": 8, "o": LB + 9}
TAIL = ({"a0": LB + 9, "w0": LB + 10, "y1": LB + 22, "q1": LB + 26},
        {"a1": LB + 10, "w1": LB + 13, "y2": LB + 18,
         "f0": LB + 20, "f1": LB + 20, "f2": LB + 22, "f3": LB + 22,
         "p0": LB + 24, "p1": LB + 26, "p2": LB + 29, "p3": LB + 32})
PV_AT = 3
EV_AT = 3
LN_AT = (2, 7, 10)
WRITE_AT = 6


def timeline():
    ops = [(-1, n, 0) for n in ("k0", "q0", "v0", "v1", "v2", "v3", "k1_0", "k1_1", "flag")]
    ops.append((BIAS_AT, "c0", 0))
    for b in range(1, B):
        ops += [((b - 1) * BATCH_STEPS * BANKS + t + (SECOND if b == 1 and n[:2] != "k1" else 0), n, b) for n, t in NEW.items()]
    last = [(STEPS * n + STEPS - 1) * BANKS for n in range(len(UNITS))]
    for n, t in enumerate(last):
        ops += [(t + at, name, n) for name, at in WHEN.items()]
    for b in range(B):
        for layer in range(2):
            t = last[layer * L1_FIRST + (b + 1) * NU[layer] - 1]
            ops += [(t + at, name, b) for name, at in TAIL[layer].items()]
    return sorted(ops, key=lambda o: o[0])


OPS = timeline()
AT = {(n, b): t for t, n, b in OPS}
PLACE = {(n, b): (i % 2, i // 2) for i, (_, n, b) in enumerate(OPS)}
END = max(AT.values()) + 1
EVACUATE = [(STEPS * n + STEPS - 1 + LAG + 1) * BANKS + EV_AT for n in range(len(UNITS))]
MASKS_AT = [BANKS * t for t in (5, 7, 9, 11, 20, 21)]
SPLITS = [(AT[n, b], n, b) for _, n, b in OPS if n in ("k0", "q0", "k1_0", "k1_1", "q1")]
SPLIT = {(n, b): i for i, (_, n, b) in enumerate(SPLITS)}


def halves(i):
    return C if SPLITS[i][1][0] == "q" else 1


def ops_at(t, names=None):
    return [(n, b) for s, n, b in OPS if s == t and (names is None or n in names)]


COL = {}
for _n, _w in (("bq0", C), ("bk0", 1), ("bv0", C), ("bq1", C), ("bk1", C), ("bv1", C), ("ln1w", C), ("ln1b", C),
               ("ln2w", C), ("ln2b", C), ("fcb", FT)):
    COL[_n] = (sum(w for _, w in COL.values()), _w)
NCOL = sum(w for _, w in COL.values())
ROW = {n: i for i, n in enumerate(("bo", "gamma", "beta", "cb", "pb"))}


def build(nc, xT, x, ctxT, mask, keymask, keymaskT, Wq0, Wk0, Wv, Wo0, Wq1, Wk1, Wc1, fcw, pjw, cols, rows, eye, out):
    with ExitStack() as ctx:
        def sb(name, shape, dt=F32):
            return ctx.enter_context(nc.sbuf_tensor(name, shape, dt))

        def sem(name):
            return ctx.enter_context(nc.semaphore(name))

        wq0 = sb("wq0", [P, C, D])
        wk0 = sb("wk0", [P, C, KF[0]])
        wv = sb("wv", [P, C, KF[0] + KF[1]])
        wo0 = sb("wo0", [P, C, D])
        wq1 = sb("wq1", [P, C, D])
        wk1 = sb("wk1", [P, C, D])
        wc1 = sb("wc1", [P, C, D])
        wmlp = sb("wmlp", [P, C * INNER + FT * D])
        wfc = wmlp[:, 0:C * INNER].rearrange("p (c n) -> p c n", c=C)
        wpj = wmlp[:, C * INNER:].rearrange("p (f n) -> p f n", f=FT)
        mk = wmlp[:, 0:B * QT * LK].rearrange("p (t k) -> p t k", k=LK)
        col = sb("col", [P, NCOL])
        row = sb("row", [P, len(ROW), D])
        ident = sb("ident", [P, P])
        identb = sb("identb", [P, P], BF16)
        colq = sb("colq", [P, 2, C])
        c0 = sb("c0", [P, 2, D])
        halfm = sb("halfm", [P, QT])
        ones = sb("ones", [P, LK], BF16)
        zeros = sb("zeros", [P, LQ], BF16)
        mkp = sb("mkp", [P, B, 3, QT, LK], BF16)
        mabs = sb("mabs", [P, 1])
        flag = sb("flag", [1, 1])
        kmrow8 = sb("kmrow8", [B, LK], U8)
        kmrow = sb("kmrow", [B, LK], BF16)
        kmcol8 = sb("kmcol8", [P, B * KT], U8)
        kmcol = sb("kmcol", [P, B * KT])
        cxT = sb("cxT", [P, C, LK])
        xTs = sb("xTs", [P, C, LQ])
        xs = sb("xs", [P, QT, D])
        xr = xs
        pf = sb("pf", [P, 2, LK])
        parts = sb("parts", [P, 2, 3, LK], BF16)
        ks0 = sb("ks0", [P, NG[0], LK], BF16)
        qs0 = sb("qs0", [P, NH[0], LQ], BF16)
        ks1 = sb("ks1", [P, 2, UH, LK], BF16)
        qs1 = sb("qs1", [P, 2, UH, LQ], BF16)
        vs = (sb("vs0", [P, B, KT, NG[0], HD[0] + 1]), sb("vs1", [P, B, KT, NG[1], HD[1] + 1]))
        mx = sb("mx", [P, 2, 2 * UH])
        mres = sb("mres", [2 * UH, 2, P])
        mparts = sb("mparts", [2 * UH, 2, 3, P], BF16)
        pt = sb("pt", [P, 3, BANKS, LK])
        oT = sb("oT", [P, 2, LK])
        rec = sb("rec", [P, 2, 2, QT, 4])
        att = sb("att", [P, QT, D])
        fT = sb("fT", [P, C, LQ])
        h0 = sb("h0", [P, QT, D])
        z = sb("z", [P, QT, D])
        x1 = h0
        res = sb("res", [P, B, QT, D])
        h1 = h0
        st6 = sb("st6", [P, QT, 6])
        mv = sb("mv", [P, 3, QT, 2])
        ve = sb("ve", [P, 3, QT])
        rstd = sb("rstd", [P, 3, QT])
        g = sb("g", [P, FT, LQ])
        bvb = g[:, 0:2, :].rearrange("p l (c m) -> p l c m", c=C)
        y = z

        sc = [ctx.enter_context(nc.psum_tensor(f"sc{i}", [P, LK], F32)) for i in range(SR)]
        stb = [ctx.enter_context(nc.psum_tensor(f"st{i}", [P, LK], F32)) for i in range(TR)]
        outp = ctx.enter_context(nc.psum_tensor("outp", [P, LK], F32))
        misc = [ctx.enter_context(nc.psum_tensor(f"misc{i}", [P, LK], F32)) for i in range(2)]

        D_ROWS = (PROD[0], MASK_ROW + 1)
        kd = tuple(nc.dram_tensor(f"kd{l}", [B, D_ROWS[l], NG[l], LK], BF16).ap() for l in range(2))
        qd = tuple(nc.dram_tensor(f"qd{l}", [B, D_ROWS[l], NH[l], LQ], BF16).ap() for l in range(2))

        WIDE = UH * LK + UH * LQ
        spare = mkp[:].rearrange("p b s t k -> p (b s t k)")

        def stack_slot(n):
            layer, _, u = UNITS[n]
            return u if layer == 0 else NU[0] + (n - L1_FIRST) % CS

        def stack_use(n):
            layer, b, _ = UNITS[n]
            return b if layer == 0 else (n - L1_FIRST) // CS

        def queries_of(n):
            layer, _, u = UNITS[n]
            if layer == 0:
                return qs0[:, u * UH:(u + 1) * UH, :]
            s = (n - L1_FIRST) % CS
            if s < 2:
                return qs1[:, s]
            o = (s - 2) * WIDE + UH * LK
            return spare[:, o:o + UH * LQ].rearrange("p (h t) -> p h t", h=UH)

        def keys_of(n):
            layer, _, u = UNITS[n]
            if layer == 0:
                w = UH * NG[0] // NH[0]
                return ks0[:, u * w:(u + 1) * w, :]
            s = (n - L1_FIRST) % CS
            if s < 2:
                return ks1[:, s]
            o = (s - 2) * WIDE
            return spare[:, o:o + UH * LK].rearrange("p (h t) -> p h t", h=UH)

        W_COUNT = (4, 1, 1, 3, 1, 2)
        s_w = [sem(f"weights_in{i}") for i in range(len(W_COUNT))]
        s_mask = sem("mask_in")
        s_km = sem("keymask_in")
        s_pinit = sem("pool_setup_step")
        s_kmr = sem("keymask_row_ready")
        s_dinit = sem("dve_setup_done")
        s_const = sem("consts_ready")
        s_fl = sem("mask_magnitude_ready")
        s_mkp = sem("mask_parts")
        s_ctx = sem("ctx_in")
        s_xT = sem("xT_in")
        s_x = sem("x_in")
        s_xr = sem("xr_ready")
        s_mf = [sem(f"misc_full{i}") for i in range(2)]
        s_me = [sem(f"misc_read{i}") for i in range(2)]
        s_pt = sem("parts_ready")
        s_pt0 = sem("first_parts_ready")
        s_pool = sem("pool_step")
        s_dve = sem("dve_step")
        s_wr = [sem(f"parts_written{i}") for i in range(2)]
        s_rows = sem("constant_rows_written")
        s_st = [sem(f"stack_in{i}") for i in range(NU[0] + CS)]
        s_sf = sem("scores_full")
        s_sr = sem("scores_reduced")
        s_tf = sem("shifted_full")
        s_ex = sem("exp_done")
        s_pv = sem("pv_done")
        s_oe = sem("out_evacuated")
        s_mp = sem("max_parts_ready")
        s_mi = [sem(f"max_in{i}") for i in range(2)]
        s_mv = sem("moments_ready")
        s_rs = sem("rstd_ready")
        s_z0 = sem("layer0_centred")
        s_z = sem("normed_ready")
        s_x1 = sem("x1_ready")
        s_x1r = sem("x1_biased")
        s_h1r = sem("h1_biased")
        s_out = sem("out_written")

        def full(eng, n, b):
            bank, i = PLACE[n, b]
            eng.wait_ge(s_mf[bank], i + 1)
            return misc[bank]

        def take(eng, n, b):
            bank, i = PLACE[n, b]
            if i > 0:
                eng.wait_ge(s_me[bank], i)
            return misc[bank]

        def filled(ins, n, b):
            ins.then_inc(s_mf[PLACE[n, b][0]], 1)

        def freed(ins, n, b):
            return ins.then_inc(s_me[PLACE[n, b][0]], 1)

        def emptied(eng, b, *names):
            for n in names:
                bank, i = PLACE[n, b]
                eng.wait_ge(s_me[bank], i + 1)

        class Chain:
            def __init__(self, s):
                self.s, self.k = s, 0

            def link(self, eng, ins):
                ins.then_inc(self.s, 1)
                self.k += 1
                eng.wait_ge(self.s, self.k)

        def await_(eng, s, value):
            if value > 0:
                eng.wait_ge(s, value)

        def write_count(i):
            return sum(16 * PAIRS for k in range(i % 2, i + 1, 2))

        norms = sorted([(AT["w0", b], 0, b) for b in range(B)] + [(AT["w0", b] + LN_AT[1], 1, b) for b in range(B)]
                       + [(AT["w1", b], 2, b) for b in range(B)])
        NORM = {(i, b): k for k, (_, i, b) in enumerate(norms)}
        ZS = {nb: k for k, nb in enumerate([(n, b) for _, n, b in OPS if n in ("y1", "y2")])}

        FIRST = 2

        def parts_made(eng, i):
            if i < FIRST:
                eng.wait_ge(s_pt0, i + 1)
            else:
                eng.wait_ge(s_pt, i - FIRST + 1)

        def split(eng, chain, i):
            _, name, b = SPLITS[i]
            s, r = i % 2, KF[0] if name == "k0" else P
            emptied(eng, b, name)
            a, p3 = pf[0:r, s, :], parts[0:r, s]
            chain.link(eng, eng.tensor_tensor(a, a, p3[:, 0], ALU.subtract))
            chain.link(eng, eng.tensor_copy(p3[:, 1], a))
            eng.tensor_tensor(p3[:, 2], a, p3[:, 1], ALU.subtract).then_inc(s_pt0 if i < FIRST else s_pt, 1)

        def mask_split(eng, b):
            eng.wait_ge(s_mkp, (b + 1) * QT)

        def c1(n, c=0, rows=P):
            k = COL[n][0] + c
            return col[0:rows, k:k + 1]

        def rowb(n):
            return row[:, ROW[n]:ROW[n] + 1, :].to_broadcast([P, QT, D])

        block = ctx.enter_context(nc.Block())

        @block.sync
        def _(sp):
            def load_ctx(b):
                sp.dma_start(cxT[:], ctxT[b:b + 1].rearrange("o (c p) k -> p (o c) k", p=P)).then_inc(s_ctx, 16)

            def load_xT(b):
                sp.dma_start(xTs[:], xT[b:b + 1].rearrange("o (c p) q -> p (o c) q", p=P)).then_inc(s_xT, 16)

            def load_x(b):
                sp.dma_start(xs[:], x[b:b + 1].rearrange("o (t p) d -> p (o t) d", p=P)).then_inc(s_x, 16)

            def write(i):
                _, n, b = SPLITS[i]
                layer = int(n[1])
                d = HD[layer]
                if n[0] == "k":
                    dst, part_of, width = kd[layer], K_PART, LK
                    h0_, nh = (0, NG[0]) if layer == 0 else (int(n[-1]) * 8, 8)
                else:
                    dst, part_of, width = qd[layer], Q_PART, LQ
                    h0_, nh = 0, P // d
                parts_made(sp, i)
                for k in range(PAIRS):
                    n = nh * halves(i)
                    to = dst[b:b + 1, k * d:(k + 1) * d, h0_:h0_ + n, :].rearrange("o d (c h) t -> (o h) d c t", h=nh)
                    sp.dma_start(to, parts[0:nh * d, i % 2, part_of[k], :].rearrange("p (c t) -> p c t", t=width)
                                 ).then_inc(s_wr[i % 2], 16)

            def written(*names):
                for key in names:
                    i = SPLIT[key]
                    sp.wait_ge(s_wr[i % 2], write_count(i))

            def read(n):
                layer, b, u = UNITS[n]
                R = D_ROWS[layer]
                if layer == 0:
                    written(("k0", b), ("q0", b))
                    if b > 0:
                        sp.wait_ge(s_tf, (n - NU[0] + 1) * STEPS * BANKS)
                    else:
                        sp.wait_ge(s_dinit, 1)
                        sp.wait_ge(s_pinit, 3)
                    w = UH * NG[0] // NH[0]
                else:
                    if n == L1_FIRST:
                        sp.wait_ge(s_rows, 64)
                    written((f"k1_{u}", b), ("q1", b))
                    c = n - L1_FIRST
                    if c >= CS:
                        sp.wait_ge(s_tf, (n - CS + 1) * STEPS * BANKS)
                    elif c >= 2:
                        mask_split(sp, (c - 1) * (B // 2) - 1)
                        sp.wait_ge(s_tf, (c - 1) * (B // 2) * BATCH_STEPS * BANKS)
                    w = UH
                s = s_st[stack_slot(n)]
                sp.dma_start(keys_of(n)[0:R], kd[layer][b:b + 1, 0:R, u * w:(u + 1) * w, :]
                             .rearrange("o r h t -> (o r) h t")).then_inc(s, 16)
                sp.dma_start(queries_of(n)[0:R], qd[layer][b:b + 1, 0:R, u * UH:(u + 1) * UH, :]
                             .rearrange("o r h t -> (o r) h t")).then_inc(s, 16)

            def max_rows(n):
                sp.wait_ge(s_mp, n + 1)
                if UNITS[n][0] == 1:
                    sp.wait_ge(s_sf, (n + 1) * STEPS * BANKS)
                for i in range(3):
                    r = M_ROW + i
                    sp.dma_start(queries_of(n)[r:r + 1], mparts[:, n % 2, i, :]).then_inc(s_mi[n % 2], 16)

            def constant_rows():
                n1 = 3 * NG[1]
                sp.wait_ge(s_dinit, 1)
                sp.wait_ge(s_kmr, 1)
                sp.dma_start(kd[1][:, M_ROW:MASK_ROW].rearrange("b r h t -> (r h) b t"),
                             ones[0:n1].unsqueeze(1).to_broadcast([n1, B, LK])).then_inc(s_rows, 16)
                sp.dma_start(kd[1][:, MASK_ROW:MASK_ROW + 1].rearrange("b r h t -> b (r h) t"),
                             kmrow[:].unsqueeze(1).to_broadcast([B, NG[1], LK])).then_inc(s_rows, 16)
                sp.dma_start(qd[1][:, M_ROW:MASK_ROW].rearrange("b r h t -> (r h) b t"),
                             zeros[0:n1].unsqueeze(1).to_broadcast([n1, B, LQ])).then_inc(s_rows, 16)
                sp.dma_start(qd[1][:, MASK_ROW:MASK_ROW + 1].rearrange("b r h t -> (r h) b t"),
                             ones[0:NH[1], 0:LQ].unsqueeze(1).to_broadcast([NH[1], B, LQ])).then_inc(s_rows, 16)

            def read_at(n):
                layer, b, u = UNITS[n]
                c = n - L1_FIRST
                if layer == 0:
                    if b == 0:
                        return -1
                    used = (n - NU[0] + 1) * STEPS
                else:
                    used = (n - CS + 1) * STEPS if c >= CS else (c - 1) * (B // 2) * BATCH_STEPS if c >= 2 else 0
                free = (used + LAG) * BANKS
                return free if layer == 0 else max(free, AT["q1", b] + 4 * BANKS + 2 * BANKS * u)

            def load(i, tile, src):
                sp.dma_start(tile[:], src).then_inc(s_w[i], 16)

            load_ctx(0)
            load_xT(0)
            sp.wait_ge(s_w[0], 16 * W_COUNT[0])
            sp.dma_start(mk, mask.rearrange("b (t p) k -> p (b t) k", p=P)).then_inc(s_mask, 16)
            load(2, wk1, Wk1.rearrange("(c p) n -> p c n", p=P))
            for i in range(FIRST):
                write(i)
            for n in range(NU[0]):
                read(n)
            full(sp, "k1_1", 0)
            load_ctx(1)
            load_xT(1)
            load(3, wo0, Wo0.rearrange("(c p) n -> p c n", p=P))
            load(3, wc1, Wc1.rearrange("(c p) n -> p c n", p=P))
            load(3, row, rows.to_broadcast([P, len(ROW), D]))
            load_x(0)
            load(4, wq1, Wq1.rearrange("(c p) n -> p c n", p=P))
            for i, (at, _, _) in enumerate(SPLITS):
                if at == -1 and i >= FIRST:
                    write(i)
            for k in range(END + 1):
                for n, b in ops_at(k, ("m",)):
                    max_rows(b)
                for i, (at, _, _) in enumerate(SPLITS):
                    if at >= 0 and at + WRITE_AT == k:
                        write(i)
                for n in range(len(UNITS)):
                    if read_at(n) == k:
                        read(n)
                for n, b in ops_at(k - 1) if k > 0 else ():
                    if n == "k1_1" and b < B - 1:
                        full(sp, n, b)
                        load_ctx(b + 1)
                        load_xT(b + 1)
                    if n == "w0" and b < B - 1:
                        emptied(sp, b, n)
                        load_x(b + 1)
                    if n == f"p{QT * C - 1}":
                        emptied(sp, b, n)
                        sp.dma_start(out[b:b + 1].rearrange("o (t p) d -> p (o t) d", p=P), y[:]).then_inc(s_out, 16)
                if k == (BATCH_STEPS - 2) * BANKS:
                    constant_rows()
                if k == (2 * BATCH_STEPS - 2) * BANKS:
                    mask_split(sp, B - 1)
                    sp.dma_start(wfc, fcw.rearrange("(c p) n -> p c n", p=P)).then_inc(s_w[5], 16)
                    sp.dma_start(wpj, pjw.rearrange("(c p) n -> p c n", p=P)).then_inc(s_w[5], 16)
            sp.wait_ge(s_out, 16 * B)

        @block.gpsimd
        def _(pool):
            chain = Chain(s_pool)
            setup = Chain(s_pinit)
            setup.link(pool, pool.memset(halfm[:], -0.5))
            setup.link(pool, pool.memset(ks0[0:M_ROW], 0.0))
            setup.link(pool, pool.memset(ks0[M_ROW:M_ROW + 3], 1.0))
            for l in range(2):
                setup.link(pool, pool.memset(vs[l][:].rearrange("p b t h d -> p (b t h) d")[:, :, HD[l]:HD[l] + 1], 1.0))
            pool.wait_ge(s_w[0], 16 * W_COUNT[0])
            for l, n in enumerate(("bq0", "bq1")):
                k = COL[n][0]
                last = pool.tensor_scalar(colq[:, l, :], col[:, k:k + C], SCALE[l], None, ALU.mult)
            last.then_inc(s_const, 1)

            def masks():
                pool.wait_ge(s_km, 32)
                setup.link(pool, pool.tensor_scalar(kmcol[:], kmcol8[:], FAR, -FAR, ALU.mult, ALU.add))
                pool.tensor_scalar(kmrow[:], kmrow8[:], FAR, -FAR, ALU.mult,
                                   ALU.add).then_inc(s_kmr, 1)
                pool.wait_ge(s_kmr, 1)

            def biases():
                for l, n in enumerate(("bv0", "bv1")):
                    for c in range(C):
                        last = pool.tensor_copy(bvb[:, l, c, :], c1(n, c).to_broadcast([P, P]))
                last.then_inc(s_const, 1)

            def split_maxima(n):
                s = n % 2
                emptied(pool, n, "m")
                a, p3 = mres[:, s, :], mparts[:, s]
                chain.link(pool, pool.tensor_tensor(a, a, p3[:, 0, :], ALU.subtract))
                chain.link(pool, pool.tensor_copy(p3[:, 1, :], a))
                pool.tensor_tensor(p3[:, 2, :], a, p3[:, 1, :], ALU.subtract).then_inc(s_mp, 1)

            def inv_std(b, i):
                pool.wait_ge(s_mv, NORM[i, b] + 1)
                chain.link(pool, pool.tensor_scalar(ve[:, i, :], mv[:, i, :, 1], EPS[i], None, ALU.add))
                pool.tensor_tensor(rstd[:, i, :], ve[:, i, :], halfm[:], ALU.pow).then_inc(s_rs, 1)

            def add_bias(b):
                emptied(pool, 0, "c0")
                pool.wait_ge(s_x, 16 * (b + 1))
                pool.tensor_tensor(xr[:], xs[:], c0[:, 0:1, :].to_broadcast([P, QT, D]), ALU.add).then_inc(s_xr, 1)

            for i, (at, _, _) in enumerate(SPLITS):
                if at == -1 and i >= FIRST:
                    split(pool, chain, i)
            biases()
            pool.tensor_copy(identb[:], ident[:]).then_inc(s_const, 1)
            masks()
            for k in range(END):
                for n, b in ops_at(k):
                    if n == "m":
                        split_maxima(b)
                    if n == "w0":
                        inv_std(b, 0)
                    if n == "w1":
                        inv_std(b, 2)
                        emptied(pool, b, "w1")
                        pool.tensor_tensor(res[:, b], h1[:], row[:, ROW["pb"]:ROW["pb"] + 1, :].to_broadcast([P, QT, D]),
                                           ALU.add).then_inc(s_h1r, 1)
                for n, b in ops_at(k - LN_AT[0], ("w0",)):
                    pool.wait_ge(s_z0, b + 1)
                    chain.link(pool, pool.tensor_tensor(h0[:], z[:], rowb("gamma"), ALU.mult))
                    pool.tensor_tensor(x1[:], h0[:], rowb("beta"), ALU.add).then_inc(s_x1, 1)
                    pool.wait_ge(s_x1, b + 1)
                    pool.tensor_tensor(res[:, b], x1[:], c0[:, 1:2, :].to_broadcast([P, QT, D]),
                                       ALU.add).then_inc(s_x1r, 1)
                for n, b in ops_at(k - LN_AT[1], ("w0",)):
                    inv_std(b, 1)
                for i, (at, _, _) in enumerate(SPLITS):
                    if at == k:
                        split(pool, chain, i)
                b, at = k // (BATCH_STEPS * BANKS), k % (BATCH_STEPS * BANKS)
                if b < B and at == (BATCH_STEPS - 2) * BANKS:
                    add_bias(b)
        @block.vector
        def _(dve):
            chain = Chain(s_dve)
            dve.memset(ones[:], 1.0)
            dve.memset(zeros[:], 0.0)
            dve.memset(outp[:], 0.0)
            dve.memset(qs0[0:M_ROW], 0.0).then_inc(s_dinit, 1)

            def split_mask(i):
                m, p3 = mk[:, i, :], mkp[:, i // QT, :, i % QT, :]
                chain.link(dve, dve.tensor_scalar(m, m, -FAR, FAR, ALU.max, ALU.min))
                chain.link(dve, dve.tensor_copy(p3[:, 0], m))
                chain.link(dve, dve.tensor_tensor(m, m, p3[:, 0], ALU.subtract))
                chain.link(dve, dve.tensor_copy(p3[:, 1], m))
                dve.tensor_tensor(p3[:, 2], m, p3[:, 1], ALU.subtract).then_inc(s_mkp, 1)

            def find_mask():
                dve.wait_ge(s_mask, 16)
                dve.tensor_reduce(mabs[:], mk, AX.XY, ALU.max, apply_absolute_value=True).then_inc(s_fl, 1)
                m = full(dve, "flag", 0)
                freed(dve.tensor_reduce(flag[:], m[0:1, 0:P], AX.X, ALU.max), "flag", 0)
                dve.wait_ge(s_fl, 1)
                for t in range(QT):
                    split_mask(t)

            def biases():
                m = full(dve, "c0", 0)
                for l, n in enumerate(("bo", "cb")):
                    ins = dve.tensor_tensor(c0[:, l, :], m[:, l * D:(l + 1) * D], row[:, ROW[n], :], ALU.add)
                freed(ins, "c0", 0)

            def maxima(k):
                n, c = k // (2 * UH), k % (2 * UH)
                dve.wait_ge(s_sf, k + 1)
                dve.tensor_reduce(mx[:, n % 2, c:c + 1], sc[k % SR][:], AX.X, ALU.max,
                                  negate=True).then_inc(s_sr, 1)

            def normalise(n):
                layer, b, u = UNITS[n]
                d = HD[layer]
                m = full(dve, "o", n)
                v = m[:].rearrange("p (h t j w) -> p h t j w", h=2, t=QT, w=VW)
                r = rec[:, n % 2]
                chain.link(dve, dve.reciprocal(r.rearrange("p h t j -> p (h t) j"),
                                               m[:].rearrange("p (a j w) -> p a j w", a=2 * QT, w=VW)[:, :, :, d]))
                if u == 0 and n > 0:
                    full(dve, f"a{UNITS[n - 1][0]}", UNITS[n - 1][1])
                a = att[:, :, u * UH * d:(u + 1) * UH * d].rearrange("p t (j h d) -> p h t j d", h=2, d=d)
                for h in range(2):
                    ins = dve.tensor_tensor(a[:, h], v[:, h, :, :, 0:d],
                                            r[:, h].unsqueeze(3).to_broadcast([P, QT, 4, d]), ALU.mult)
                freed(ins, "o", n)

            def moments(b, i, src):
                for t in range(QT):
                    ins = dve.bn_stats(st6[:, t, :], src[:, t, :])
                chain.link(dve, ins)
                for t in range(QT):
                    ins = dve.bn_aggr(mv[:, i, t, :], st6[:, t, :])
                ins.then_inc(s_mv, 1)

            def centre(b, i, src):
                dve.wait_ge(s_rs, NORM[i, b] + 1)
                for t in range(QT):
                    ins = dve.tensor_scalar(z[:, t, :], src[:, t, :], mv[:, i, t, 0:1], rstd[:, i, t:t + 1],
                                            ALU.subtract, ALU.mult)
                return ins

            def flat(a):
                return a.rearrange("p t d -> p (t d)")

            for i in range(FIRST):
                split(dve, chain, i)
            for t in range(-1, END):
                if 0 <= t < ALL * BANKS:
                    maxima(t)
                for n, b in ops_at(t):
                    if n == "flag":
                        find_mask()
                    if n == "c0":
                        biases()
                    if n == "o":
                        normalise(b)
                    if n == "w0":
                        m = full(dve, n, b)
                        dve.wait_ge(s_xr, b + 1)
                        await_(dve, s_x1r, b)
                        freed(dve.tensor_tensor(flat(h0[:]), m[:], flat(xr[:]), ALU.add), n, b)
                        emptied(dve, b, n)
                        moments(b, 0, h0)
                    if n == "w1":
                        m = full(dve, n, b)
                        dve.wait_ge(s_x1r, B)
                        await_(dve, s_h1r, b)
                        freed(dve.tensor_tensor(flat(h1[:]), m[:], flat(res[:, b]), ALU.add), n, b)
                        emptied(dve, b, n)
                        moments(b, 2, h1)
                    if n[0] == "p":
                        m = full(dve, n, b)
                        q, c = divmod(int(n[1]), C)
                        c = slice(c * P, (c + 1) * P)
                        dve.wait_ge(s_h1r, b + 1)
                        freed(dve.tensor_tensor(y[:, q, c], m[:, 0:P], res[:, b, q, c], ALU.add), n, b)
                if t in MASKS_AT:
                    split_mask(QT + MASKS_AT.index(t))
                for n, b in ops_at(t - LN_AT[0], ("w0", "w1")):
                    if n == "w0":
                        if b > 0:
                            full(dve, "y1", b - 1)
                        centre(b, 0, h0).then_inc(s_z0, 1)
                    if n == "w1":
                        full(dve, "y2" if b else "y1", b - 1 if b else B - 1)
                        await_(dve, s_out, 16 * b)
                        centre(b, 2, h1).then_inc(s_z, 1)
                for n, b in ops_at(t - LN_AT[1], ("w0",)):
                    dve.wait_ge(s_x1, b + 1)
                    moments(b, 1, x1)
                for n, b in ops_at(t - LN_AT[2], ("w0",)):
                    centre(b, 1, x1).then_inc(s_z, 1)

        @block.scalar
        def _(act):
            def load(i, tile, src):
                act.dma_start(tile[:], src).then_inc(s_w[i], 16)

            load(0, col, cols)
            load(0, wk0, Wk0.rearrange("(c p) n -> p c n", p=P))
            load(0, wq0, Wq0.rearrange("(c p) n -> p c n", p=P))
            load(0, ident, eye)
            load(1, wv, Wv.rearrange("(c p) n -> p c n", p=P))
            act.dma_start(kmcol8[:], keymaskT).then_inc(s_km, 16)
            act.dma_start(kmrow8[:], keymask).then_inc(s_km, 16)

            def exp(k):
                s, j = k // BANKS, k % BANKS
                layer, b, _ = UNITS[s // STEPS]
                kt = s % STEPS
                act.wait_ge(s_tf, k + 1)
                if j == 0:
                    await_(act, s_pv, s - 2)
                bias = kmcol[:, b * KT + kt:b * KT + kt + 1] if layer else 0.0
                act.activation(pt[:, s % 3, j, :], stb[k % TR][:], ACT.Exp, bias=bias).then_inc(s_ex, 1)

            def evacuate(n):
                act.wait_ge(s_pv, (n + 1) * STEPS)
                if n > 1:
                    full(act, "o", n - 2)
                act.copy(oT[:, n % 2, :], outp[:]).then_inc(s_oe, 1)

            def take_values(b, t):
                m = full(act, f"v{t}", b)
                act.copy(vs[0][:, b, t, :, 0:HD[0]], m[:, 0:KF[0]].rearrange("p (g d) -> p g d", d=HD[0]))
                ins = act.copy(vs[1][:, b, t, :, 0:HD[1]],
                               m[:, KF[0]:KF[0] + KF[1]].rearrange("p (g d) -> p g d", d=HD[1]))
                freed(ins, f"v{t}", b)

            def project(name, b):
                m = full(act, name, b)
                i = SPLIT[name, b]
                s = i % 2
                r = KF[0] if name == "k0" else P
                if i > 1:
                    parts_made(act, i - 2)
                    act.wait_ge(s_wr[s], write_count(i - 2))
                for to in (parts[0:r, s, 0, :], pf[0:r, s, :]):
                    if name[0] == "q":
                        l = int(name[1])
                        for c in range(C):
                            ins = act.activation(to[:, c * LQ:(c + 1) * LQ], m[:, c * LQ:(c + 1) * LQ], ACT.Identity,
                                                 bias=colq[:, l, c:c + 1], scale=SCALE[l])
                    else:
                        bias = c1("bk0", rows=r) if name == "k0" else c1("bk1", int(name[-1]))
                        ins = act.activation(to, m[0:r, :], ACT.Identity, bias=bias)
                freed(ins, name, b)

            def take_maxima(n):
                m = full(act, "m", n)[0:2 * UH, 0:P]
                s = n % 2
                await_(act, s_mi[s], n // 2 * 48)
                act.copy(mparts[:, s, 0, :], m)
                freed(act.copy(mres[:, s, :], m), "m", n)

            def norm_affine(n, b, ln):
                m = full(act, n, b)
                for c in range(C):
                    ins = act.activation(fT[:, c, :], m[:, c * LQ:(c + 1) * LQ], ACT.Identity, bias=c1(ln + "b", c),
                                         scale=c1(ln + "w", c))
                freed(ins, n, b)

            act.wait_ge(s_const, 1)
            for t in range(-1, END):
                if t == (L1_FIRST * STEPS + LAG) * BANKS:
                    act.wait_ge(s_kmr, 1)
                if 0 <= t - LAG * BANKS < ALL * BANKS:
                    exp(t - LAG * BANKS)
                if t in EVACUATE:
                    evacuate(EVACUATE.index(t))
                for n, b in ops_at(t):
                    if (n, b) in SPLIT:
                        project(n, b)
                    if n[0] == "v":
                        take_values(b, int(n[1]))
                    if n == "m":
                        take_maxima(b)
                    if n in ("a0", "a1"):
                        m = full(act, n, b)
                        freed(act.copy(fT[:].rearrange("p c q -> p (c q)"), m[:]), n, b)
                    if n == "y1":
                        norm_affine(n, b, "ln1")
                    if n == "y2":
                        norm_affine(n, b, "ln2")
                    if n[0] == "f" and n != "flag":
                        m = full(act, n, b)
                        i = int(n[1])
                        for k in range(2):
                            ins = act.activation(g[:, 2 * i + k, :], m[:, k * LQ:(k + 1) * LQ], ACT.Gelu_apprx_tanh,
                                                 bias=c1("fcb", 2 * i + k))
                        freed(ins, n, b)

        @block.tensor
        def _(pe):
            def product(out_, pairs):
                for i, (l, r) in enumerate(pairs):
                    ins = pe.matmul(out_, l, r, start=i == 0, stop=i == len(pairs) - 1)
                return ins

            def scores(s, i, add_mask):
                n = s // STEPS
                layer, b, u = UNITS[n]
                if s % STEPS == 0 and i == 0:
                    pe.wait_ge(s_st[stack_slot(n)], 32 * (stack_use(n) + 1))
                k = s * BANKS + i
                h, t = k % (2 * UH) // QT, k % QT
                await_(pe, s_sr, k - SR + 1)
                more = add_mask and layer == 0
                R = S_ROWS[layer]
                ins = pe.matmul(sc[k % SR][:], queries_of(n)[0:R, h, t * P:(t + 1) * P],
                                keys_of(n)[0:R, h * NG[layer] // NH[layer], :], start=True, stop=not more)
                if more:
                    for p in range(3):
                        ins = pe.matmul(sc[k % SR][:], identb[:], mkp[:, b, p, t, :], start=False, stop=p == 2)
                ins.then_inc(s_sf, 1)

            def shifted(s, j, add_mask):
                n, kt = s // STEPS, s % STEPS
                layer, b, u = UNITS[n]
                if kt == 0 and j == 0:
                    pe.wait_ge(s_mi[n % 2], (n // 2 + 1) * 48)
                k = s * BANKS + j
                bank = stb[k % TR]
                await_(pe, s_ex, k - TR + 1)
                more = add_mask and layer == 0
                R = ST_ROWS
                hs = 2 if layer == 0 else 1
                for i in range(0, 2, hs):
                    h = 2 * j + i
                    ins = pe.matmul(bank[:, i * LQ:(i + hs) * LQ],
                                    keys_of(n)[0:R, h * NG[layer] // NH[layer], kt * P:(kt + 1) * P],
                                    queries_of(n)[0:R, h:h + hs, :], start=True, stop=not more)
                if more:
                    o = bank[:].rearrange("p (h t q) -> p h t q", h=2, q=P)
                    for p in range(3):
                        for t in range(QT):
                            ins = pe.matmul(o[:, :, t, :], mkp[:, b, p, t, kt * P:(kt + 1) * P],
                                            identb[:].unsqueeze(1).to_broadcast([P, 2, P]),
                                            start=False, stop=p == 2 and t == QT - 1)
                ins.then_inc(s_tf, 1)

            def values(s):
                n, kt = s // STEPS, s % STEPS
                layer, b, u = UNITS[n]
                w = HD[layer] + 1
                if n == 0 and kt == 0:
                    pe.wait_ge(s_dinit, 1)
                if kt == 0:
                    await_(pe, s_oe, n)
                    if u == 0 and layer == 0:
                        emptied(pe, b, *(f"v{t}" for t in range(KT)))
                pe.wait_ge(s_ex, (s + 1) * BANKS)
                for j in range(BANKS):
                    to = outp[VW * j:VW * j + w, :]
                    if layer == 0:
                        gs = (u * UH + 2 * j) * NG[0] // NH[0]
                        ins = pe.matmul(to, vs[0][:, b, kt, gs, :], pt[:, s % 3, j, :], start=kt == 0, stop=kt == KT - 1)
                    else:
                        for i in range(2):
                            ins = pe.matmul(to[:, i * LQ:(i + 1) * LQ], vs[1][:, b, kt, u * UH + 2 * j + i, :],
                                            pt[:, s % 3, j, i * LQ:(i + 1) * LQ],
                                            start=kt == 0 and i == 0, stop=kt == KT - 1, skip_group_check=True)
                ins.then_inc(s_pv, 1)

            def turn(m, src):
                for c in range(C):
                    for t in range(QT):
                        ins = pe.transpose(m[:, c * LQ + t * P:c * LQ + (t + 1) * P], src[:, t, c * P:(c + 1) * P], ident[:])
                return ins

            def to_model(m, w):
                for t in range(QT):
                    ins = product(m[:, t * D:(t + 1) * D], [(fT[:, c, t * P:(t + 1) * P], w[:, c, :]) for c in range(C)])
                return ins

            def queries(m, w, src):
                for o in range(C):
                    ins = product(m[:, o * LQ:(o + 1) * LQ], [(w[:, c, o * P:(o + 1) * P], src[:, c, :]) for c in range(C)])
                return ins

            def dense(n, b):
                m = take(pe, n, b)
                if n == "k0":
                    if b == 0:
                        pe.wait_ge(s_w[0], 16 * W_COUNT[0])
                    pe.wait_ge(s_ctx, 16 * (b + 1))
                    ins = product(m[0:KF[0], :], [(wk0[:, c, :], cxT[:, c, :]) for c in range(C)])
                elif n == "q0":
                    pe.wait_ge(s_xT, 16 * (b + 1))
                    ins = queries(m, wq0, xTs)
                elif n[0] == "v":
                    if b == 0:
                        pe.wait_ge(s_w[1], 16 * W_COUNT[1])
                    t = int(n[1])
                    ins = product(m[:, 0:KF[0] + KF[1]], [(cxT[:, c, t * P:(t + 1) * P], wv[:, c, :]) for c in range(C)])
                elif n[:2] == "k1":
                    if b == 0:
                        pe.wait_ge(s_w[2], 16 * W_COUNT[2])
                    o = int(n[-1])
                    ins = product(m[:], [(wk1[:, c, o * P:(o + 1) * P], cxT[:, c, :]) for c in range(C)])
                elif n == "flag":
                    pe.wait_ge(s_fl, 1)
                    ins = pe.transpose(m[0:1, 0:P], mabs[:], ident[:])
                elif n == "c0":
                    pe.wait_ge(s_const, 2)
                    pe.wait_ge(s_w[3], 16 * W_COUNT[3])
                    for l, w in enumerate((wo0, wc1)):
                        ins = product(m[:, l * D:(l + 1) * D], [(bvb[:, l, c, :], w[:, c, :]) for c in range(C)])
                elif n == "m":
                    pe.wait_ge(s_sr, (b + 1) * STEPS * BANKS)
                    ins = pe.transpose(m[0:2 * UH, 0:P], mx[:, b % 2, :], ident[:])
                elif n == "o":
                    pe.wait_ge(s_oe, b + 1)
                    for i in range(2 * QT):
                        ins = pe.transpose(m[:, i * P:(i + 1) * P], oT[:, b % 2, i * P:(i + 1) * P], ident[:])
                elif n in ("a0", "a1"):
                    layer = int(n[1])
                    first = b * NU[layer] + layer * L1_FIRST
                    for k in range(NU[layer]):
                        emptied(pe, first + k, "o")
                    ins = turn(m, att)
                elif n == "w0":
                    emptied(pe, b, "a0")
                    ins = to_model(m, wo0)
                elif n == "w1":
                    emptied(pe, b, "a1")
                    ins = to_model(m, wc1)
                elif n in ("y1", "y2"):
                    pe.wait_ge(s_z, ZS[n, b] + 1)
                    ins = turn(m, z)
                elif n == "q1":
                    if b == 0:
                        pe.wait_ge(s_w[4], 16 * W_COUNT[4])
                    emptied(pe, b, "y1")
                    ins = queries(m, wq1, fT)
                elif n[0] == "f":
                    if b == 0:
                        pe.wait_ge(s_w[5], 16 * W_COUNT[5])
                    emptied(pe, b, "y2")
                    i = int(n[1])
                    for k in range(2):
                        o = 2 * i + k
                        ins = product(m[:, k * LQ:(k + 1) * LQ], [(wfc[:, c, o * P:(o + 1) * P], fT[:, c, :]) for c in range(C)])
                else:
                    t, c = divmod(int(n[1]), C)
                    emptied(pe, b, *(f"f{i}" for i in range(FT // 2)))
                    ins = product(m[:, 0:P], [(g[:, f, t * P:(t + 1) * P], wpj[:, f, c * P:(c + 1) * P]) for f in range(FT)])
                filled(ins, n, b)

            def attention(add_mask):
                for k in range(END):
                    t, i = k // BANKS, k % BANKS
                    if add_mask and i == 0 and t % BATCH_STEPS == 0 and t < L1_FIRST * STEPS:
                        mask_split(pe, t // BATCH_STEPS)
                        pe.wait_ge(s_const, 3)
                    if t < ALL:
                        scores(t, i, add_mask)
                    if 0 <= t - LAG < ALL:
                        shifted(t - LAG, i, add_mask)
                    if i == PV_AT and 0 <= t - LAG - 1 < ALL:
                        values(t - LAG - 1)
                    for n, b in ops_at(k):
                        dense(n, b)

            for n, b in ops_at(-1):
                dense(n, b)
            emptied(pe, 0, "flag")
            masked = pe.value_load(flag[0:1, 0:1].bitcast(I32))
            with pe.If(masked != 0):
                attention(True)
            with pe.Else():
                attention(False)


def kernel(**inputs):
    import concourse.bacc as _bacc
    from concourse.bass_utils import run_bass_kernel_spmd as _run

    a = {n: np.asarray(v) for n, v in inputs.items()}
    l0 = {n[len("L0_xattn_"):]: v for n, v in a.items() if n.startswith("L0_xattn_")}
    l1 = {n[len("L1_xattn_"):]: v for n, v in a.items() if n.startswith("L1_xattn_")}

    def columns(v):
        return v.reshape(-1, P).T

    bv0 = np.repeat(l0["bv"].reshape(NG[0], 1, HD[0]), NH[0] // NG[0], axis=1).reshape(D)
    bk0 = np.concatenate([l0["bk"], np.zeros(P - KF[0], np.float32)])
    vectors = {"bq0": l0["bq"], "bk0": bk0, "bv0": bv0, "bq1": l1["q_b"], "bk1": l1["k_b"], "bv1": l1["v_b"],
               "ln1w": l1["ln1_w"], "ln1b": l1["ln1_b"], "ln2w": l1["ln2_w"], "ln2b": l1["ln2_b"], "fcb": l1["fc_b"]}
    broad = {"bo": l0["bo"], "gamma": l0["gamma"], "beta": l0["beta"], "cb": l1["cproj_b"], "pb": l1["proj_b"]}
    keymask = a["mask_BxS2_bf1"].view(np.uint8)
    arrays = {
        "xT": a["x"].transpose(0, 2, 1),
        "x": a["x"],
        "ctxT": a["ctx_2048"].transpose(0, 2, 1),
        "mask": a["mask_Bx1xSxS2_ff0"].reshape(B, LQ, LK),
        "keymask": keymask.reshape(B, LK),
        "keymaskT": keymask.reshape(B * KT, P).T,
        "Wq0": l0["Wq"], "Wk0": l0["Wk"], "Wv": np.concatenate([l0["Wv"], l1["v_w"]], axis=1), "Wo0": l0["Wo"],
        "Wq1": l1["q_w"], "Wk1": l1["k_w"], "Wc1": l1["cproj_w"], "fcw": l1["fc_w"], "pjw": l1["proj_w"],
        "cols": np.concatenate([columns(vectors[n]) for n in COL], axis=1),
        "rows": np.stack([broad[n] for n in ROW])[None],
        "eye": np.eye(P, dtype=np.float32),
    }
    arrays = {n: np.ascontiguousarray(v) for n, v in arrays.items()}
    nc = _bacc.Bacc("TRN2", target_bir_lowering=False, num_devices=1)
    args = [nc.dram_tensor(f"in_{n}", v.shape, mybir.dt.from_np(v.dtype), kind="ExternalInput").ap()
            for n, v in arrays.items()]
    out = nc.dram_tensor("out", (B, LQ, D), F32, kind="ExternalOutput").ap()
    build(nc, *args, out)
    r = _run(nc, [{f"in_{n}": v for n, v in arrays.items()}], core_ids=[0])
    return r.results[0]["out"]
```
